# Optimizing a Trainium2 kernel written in Bass

```python
import numpy as np
import jax
import jax.numpy as jnp

def _softmax(x, axis=-1):
    return jax.nn.softmax(x, axis=axis)

def _gelu(x):
    return jax.nn.gelu(x, approximate=True)

def _silu(x):
    return jax.nn.silu(x)

def _sigmoid(x):
    return jax.nn.sigmoid(x)

def _layernorm(x, axis=-1, eps=1e-05):
    m = jnp.mean(x, axis=axis, keepdims=True)
    v = jnp.var(x, axis=axis, keepdims=True)
    return (x - m) / jnp.sqrt(v + eps)

def _scatter_add(tgt, idx, src, axis=0):
    return tgt.at[idx].add(src)

def _segment_sum(src, seg, n):
    return jax.ops.segment_sum(src, seg, n)
kernel_name = 'mk_hybrid_d1_jaxref_r4_acdce0'

def setup_inputs(seed: int=0):
    np.random.seed(seed)
    _w = jnp.asarray

    def _L0_attn_a_setup():
        import jax, jax.numpy as jnp
        import numpy as np
        OFFSETS = sorted(set(range(0, 33)) | {48, 64, 96, 128, 192, 64, 96, 128, 192, 256, 384})
        B, N, D, H = (2, 512, 256, 16)
        HD = D // H

        def _shift(t, delta, n):
            if delta == 0:
                return t
            if delta >= n:
                return jnp.zeros_like(t)
            return jnp.pad(t[:, :, :n - delta], ((0, 0), (0, 0), (delta, 0), (0, 0)))
        key = jax.random.key(seed)
        ks = jax.random.split(key, 4)
        x = jax.random.normal(ks[0], (B, N, D), jnp.float32)
        Wqkv = jax.random.normal(ks[1], (D, 3 * D), jnp.float32) * D ** (-0.5)
        bqkv = jnp.zeros((3 * D,), jnp.float32)
        Wout = jax.random.normal(ks[2], (D, D), jnp.float32) * D ** (-0.5)
        bout = jnp.zeros((D,), jnp.float32)
        Wgate = jax.random.normal(ks[3], (D, D), jnp.float32) * D ** (-0.5)
        bgate = jnp.full((D,), 2.0, jnp.float32)
        alphas = np.linspace(0.2, 2.0, H, dtype=np.float32)
        deltas = np.log1p(np.asarray(OFFSETS, dtype=np.float32))
        pos_bias = jnp.asarray(-deltas[:, None] * alphas[None, :], jnp.float32)
        return dict(x=x, Wqkv=Wqkv, bqkv=bqkv, Wout=Wout, bout=bout, Wgate=Wgate, bgate=bgate, pos_bias=pos_bias)
    _L0_attn_a_in = _L0_attn_a_setup()

    def _L0_attn_b_setup():
        import jax, jax.numpy as jnp
        import numpy as np
        EMBED_DIM = 256
        NUM_HEAD = 16
        NEG_BIG = 10000000000.0
        key = jax.random.key(seed)
        k_x, k_w1, k_b1, k_w2, k_b2 = jax.random.split(key, 5)
        B, S, E = (4, 512, EMBED_DIM)
        std = 1.0 / np.sqrt(E)
        return {'x': jax.random.normal(k_x, (B, S, E), dtype=jnp.float32), 'W1': jax.random.uniform(k_w1, (E, 3 * E), dtype=jnp.float32, minval=-std, maxval=std), 'b1': jax.random.uniform(k_b1, (3 * E,), dtype=jnp.float32, minval=-std, maxval=std), 'W2': jax.random.uniform(k_w2, (E, E), dtype=jnp.float32, minval=-std, maxval=std), 'b2': jax.random.uniform(k_b2, (E,), dtype=jnp.float32, minval=-std, maxval=std)}
    _L0_attn_b_in = _L0_attn_b_setup()

    def _L0_ffn_setup():
        import jax, jax.numpy as jnp
        import numpy as np
        B, S, D, E, H, K = (64, 512, 256, 32, 1024, 8)
        key = jax.random.key(seed)
        k0, k1, k2, k3 = jax.random.split(key, 4)
        x = jax.random.normal(k0, (B, S, D), jnp.float32)
        gate_w = jax.random.normal(k1, (E, D), jnp.float32) * (1.0 / np.sqrt(D))
        gate_b = jnp.zeros((E,), jnp.float32)
        w1 = jax.random.normal(k2, (E, D + 1, H), jnp.float32) * (1.0 / np.sqrt(D + 1))
        w2 = jax.random.normal(k3, (E, H + 1, D), jnp.float32) * (1.0 / np.sqrt(H + 1))
        return {'x': x, 'gate_w': gate_w, 'gate_b': gate_b, 'w1': w1, 'w2': w2}
    _L0_ffn_in = _L0_ffn_setup()
    _d = {'L0_attn_a_x': _L0_attn_a_in['x'], 'L0_attn_a_Wqkv': _L0_attn_a_in['Wqkv'], 'L0_attn_a_bqkv': _L0_attn_a_in['bqkv'], 'L0_attn_a_Wout': _L0_attn_a_in['Wout'], 'L0_attn_a_bout': _L0_attn_a_in['bout'], 'L0_attn_a_Wgate': _L0_attn_a_in['Wgate'], 'L0_attn_a_bgate': _L0_attn_a_in['bgate'], 'L0_attn_a_pos_bias': _L0_attn_a_in['pos_bias'], 'L0_attn_b_W1': _L0_attn_b_in['W1'], 'L0_attn_b_b1': _L0_attn_b_in['b1'], 'L0_attn_b_W2': _L0_attn_b_in['W2'], 'L0_attn_b_b2': _L0_attn_b_in['b2'], 'L0_ffn_gate_w': _L0_ffn_in['gate_w'], 'L0_ffn_gate_b': _L0_ffn_in['gate_b'], 'L0_ffn_w1': _L0_ffn_in['w1'], 'L0_ffn_w2': _L0_ffn_in['w2']}
    _x0 = _d['L0_attn_a_x']
    _d['L0_attn_a_x'] = jax.random.normal(jax.random.fold_in(jax.random.key(seed), 1), (8, 1024, 256), dtype=_x0.dtype)
    del _x0
    return _d

def reference(L0_attn_a_x, L0_attn_a_Wqkv, L0_attn_a_bqkv, L0_attn_a_Wout, L0_attn_a_bout, L0_attn_a_Wgate, L0_attn_a_bgate, L0_attn_a_pos_bias, L0_attn_b_W1, L0_attn_b_b1, L0_attn_b_W2, L0_attn_b_b2, L0_ffn_gate_w, L0_ffn_gate_b, L0_ffn_w1, L0_ffn_w2):

    def _L0_attn_a_ref(x, Wqkv, bqkv, Wout, bout, Wgate, bgate, pos_bias):
        import jax, jax.numpy as jnp
        import numpy as np
        OFFSETS = sorted(set(range(0, 33)) | {48, 64, 96, 128, 192, 64, 96, 128, 192, 256, 384})
        B, N, D, H = (2, 512, 256, 16)
        HD = D // H

        def _shift(t, delta, n):
            if delta == 0:
                return t
            if delta >= n:
                return jnp.zeros_like(t)
            return jnp.pad(t[:, :, :n - delta], ((0, 0), (0, 0), (delta, 0), (0, 0)))
        b, n, d = x.shape
        scale = HD ** (-0.5)
        qkv = x @ Wqkv + bqkv
        q, k, v = jnp.split(qkv, 3, axis=-1)
        q = q.reshape(b, n, H, HD).transpose(0, 2, 1, 3)
        k = k.reshape(b, n, H, HD).transpose(0, 2, 1, 3)
        v = v.reshape(b, n, H, HD).transpose(0, 2, 1, 3)
        scores = jnp.stack([jnp.einsum('bhnd,bhnd->bhn', q, _shift(k, delta, n)) for delta in OFFSETS], axis=-1) * scale
        scores = scores + pos_bias.T[None, :, None, :]
        invalid = jnp.arange(n)[:, None] < jnp.asarray(OFFSETS)[None, :]
        scores = jnp.where(invalid[None, None], -jnp.inf, scores)
        alpha = jax.nn.softmax(scores, axis=-1)
        out = jnp.zeros_like(q)
        for i, delta in enumerate(OFFSETS):
            out = out + alpha[..., i:i + 1] * _shift(v, delta, n)
        flat = out.transpose(0, 2, 1, 3).reshape(b, n, d)
        gate = jax.nn.sigmoid(x @ Wgate + bgate)
        return flat * gate @ Wout + bout

    def _L0_attn_b_ref(x, W1, b1, W2, b2):
        import jax, jax.numpy as jnp
        import numpy as np
        EMBED_DIM = 256
        NUM_HEAD = 16
        NEG_BIG = 10000000000.0
        B, S, E = x.shape
        H = NUM_HEAD
        y = jnp.einsum('bse,ef->bsf', x, W1) + b1
        y = y.reshape(B, S, H, -1).transpose(0, 2, 1, 3)
        q, k, v = jnp.split(y, 3, axis=-1)
        dk = jnp.asarray(v.shape[-1], x.dtype) ** 0.5
        w = jnp.einsum('bhqd,bhkd->bhqk', q, k) / dk
        mask = jnp.tril(jnp.ones((S, S), dtype=x.dtype))
        w = w * mask - NEG_BIG * (1.0 - mask)
        w = jax.nn.softmax(w, axis=-1)
        attn = jnp.einsum('bhqk,bhkd->bhqd', w, v)
        attn = attn.transpose(0, 2, 1, 3).reshape(B, S, E)
        return jnp.einsum('bse,ef->bsf', attn, W2) + b2

    def _L0_ffn_ref(x, gate_w, gate_b, w1, w2):
        import jax, jax.numpy as jnp
        import numpy as np
        B, S, D, E, H, K = (64, 512, 256, 32, 1024, 8)
        b, s, d = x.shape
        logits = jnp.einsum('bsd,ed->bse', x, gate_w) + gate_b
        probs = jax.nn.softmax(logits, axis=-2)
        vals_t, idx_t = jax.lax.top_k(probs.transpose(0, 2, 1), K)
        vals = vals_t.transpose(0, 2, 1)
        idx = idx_t.transpose(0, 2, 1)
        flat_idx = idx.reshape(b, K * E)
        tok = jnp.take_along_axis(x, flat_idx[:, :, None], axis=1)
        tok = tok.reshape(b, K, E, d)
        merged = jnp.einsum('bked,bke->bed', tok, vals)
        ones = jnp.ones(merged.shape[:-1] + (1,), merged.dtype)
        h = jnp.einsum('bei,eih->beh', jnp.concatenate([merged, ones], -1), w1)
        h = jax.nn.gelu(h, approximate=False)
        o = jnp.einsum('bej,ejo->beo', jnp.concatenate([h, ones], -1), w2)
        out_tok = jnp.einsum('beo,bke->bkeo', o, vals).reshape(b, K * E, d)
        out = jnp.zeros_like(x).at[jnp.arange(b)[:, None], flat_idx].add(out_tok)
        return out
    x = L0_attn_a_x
    x = x + _L0_attn_a_ref(_layernorm(x, axis=-1), L0_attn_a_Wqkv, L0_attn_a_bqkv, L0_attn_a_Wout, L0_attn_a_bout, L0_attn_a_Wgate, L0_attn_a_bgate, L0_attn_a_pos_bias)
    x = x + _L0_ffn_ref(_layernorm(x, axis=-1), L0_ffn_gate_w, L0_ffn_gate_b, L0_ffn_w1, L0_ffn_w2)
    x = x + _L0_attn_b_ref(_layernorm(x, axis=-1), L0_attn_b_W1, L0_attn_b_b1, L0_attn_b_W2, L0_attn_b_b2)
    x = x + _L0_ffn_ref(_layernorm(x, axis=-1), L0_ffn_gate_w, L0_ffn_gate_b, L0_ffn_w1, L0_ffn_w2)
    return x

_drawn_inputs = setup_inputs


def setup_inputs(seed=0):
    import zlib

    import numpy as np

    out = dict(_drawn_inputs(seed))
    spreads = {'L0_attn_a_bqkv': (0.0, 0.1),
     'L0_attn_a_bout': (0.0, 0.1),
     'L0_attn_a_bgate': (2.0, 0.6),
     'L0_ffn_gate_b': (0.0, 0.8)}
    factors = {'L0_attn_b_b1': 2.769}
    for name, (base, spread) in spreads.items():
        noise = np.random.default_rng([zlib.crc32(name.encode()), seed]).standard_normal(out[name].shape)
        drawn = base * np.exp(spread * noise) if base else spread * noise
        out[name] = jnp.asarray(drawn.astype(out[name].dtype))
    for name, factor in factors.items():
        out[name] = (out[name] * factor).astype(out[name].dtype)
    return out
```

```python
from contextlib import ExitStack

import concourse.bass as bass
from concourse import mybir

P = 128
F32 = mybir.dt.float32
BF16 = mybir.dt.bfloat16
ALU = mybir.AluOpType
ACT = mybir.ActivationFunctionType
AX = mybir.AxisListType

B, N, D = 8, 1024, 256
NT = N // P
KD = D // P
H, HD = 16, 16
G, HG = 4, 4
NE, HE, TOPK = 32, 1024, 8
EPS = 1e-5
NEG = -1e30
LOWEST = -3e38
OFFSETS = sorted(set(range(33)) | {48, 64, 96, 128, 192, 256, 384})
SPAN = 512
LINE = SPAN + P


def window(ap, h):
    return bass.AP(ap.tensor, h * P * LINE + P - 1, [[LINE - 1, P], [1, SPAN]])


def at_iteration(b, count):
    if isinstance(b, int):
        return count(b)
    first, second = count(1), count(2)
    return b * (second - first) + (first - (second - first))


def wait_alone(eng, sem, b, count, passed):
    wait(eng, sem, b, count)
    if not isinstance(b, int):
        eng.sem_inc(passed, 1)


def wait(eng, sem, b, count):
    value = at_iteration(b, count)
    if isinstance(b, int) and not value:
        return
    eng.wait_ge(sem, value)



def build_constants(nc, ident, x, x_sb):
    with nc.semaphore("x_loaded") as x_loaded, nc.semaphore("ident_steps") as ident_steps, nc.Block() as block:
        @block.sync
        def _(sp):
            for b in range(B):
                sp.dma_start(x_sb[:, b * NT:(b + 1) * NT, :],
                             x[b].rearrange("(i p) d -> p i d", p=P)).then_inc(x_loaded, 16)
            sp.wait_ge(x_loaded, 16 * B)

        @block.gpsimd
        def _(pool):
            pool.memset(ident[:, :], 0.0).then_inc(ident_steps, 1)
            pool.wait_ge(ident_steps, 1)
            pool.affine_select(out=ident[:, :], in_=ident[:, :], compare_op=ALU.not_equal, fill=1.0, base=0,
                               pattern=[[-1, P]], channel_multiplier=1).then_inc(ident_steps, 1)
            pool.wait_ge(ident_steps, 2)


def layer_norm_stats(dve, act_sem, dve_sem, x_sb, stats, mv, std, rstd):
    done = 0
    for t in range(B * NT):
        dve.bn_stats(stats[:, t, :], x_sb[:, t, :]).then_inc(dve_sem, 1)
    done += B * NT
    dve.wait_ge(dve_sem, done)
    for t in range(B * NT):
        dve.bn_aggr(mv[:, t, :], stats[:, t, :]).then_inc(dve_sem, 1)
    done += B * NT
    dve.wait_ge(dve_sem, done)
    dve.tensor_scalar(std[:, :], mv[:, :, 1], EPS, None, ALU.add).then_inc(dve_sem, 1)
    done += 1
    dve.wait_ge(act_sem, 1)
    dve.reciprocal(rstd[:, :], std[:, :]).then_inc(dve_sem, 1)
    return done


STATS_STEPS = 2 * B * NT + 1



def attention_schedule(banded):
    def prep(g):
        out = [("q", g, 0), ("q", g, 1), ("k", g, 0), ("k", g, 1)]
        for h in range(HG):
            for i in range(NT):
                chunks = 1 if banded or i < 4 else 2
                out += [("mx", g, h, i, c) for c in range(chunks)]
        return out + [("mred", g), ("mt", g, 0), ("mt", g, 1)]

    def tokens():
        out = []
        for i2 in range(NT // 2):
            out += [("z", i2), ("zt", i2)]
        return out

    def outputs():
        out = [("ot", 3, 0), ("ot", 3, 1)] + ([("gmul",)] if banded else [])
        return out + [("at", 0), ("at", 1), ("op", 0), ("at", 2), ("op", 1), ("at", 3), ("op", 2), ("op", 3)]

    def body(b):
        out = []
        pending = []
        lag = 1 if banded else 2
        for g in range(G):
            if g == 0:
                extras = (outputs() if b else [])
                if banded:
                    extras += [("gate", i2) for i2 in range(NT // 2)]
                extras += prep(1)
            elif g < 3:
                extras = [("ot", g - 1, 0), ("ot", g - 1, 1)] + prep(g + 1)
            else:
                extras = [("ot", 2, 0), ("ot", 2, 1)] + (tokens() + prep(4) if b < B - 1 else [])
            slots = HG * NT
            taken = 0
            for s in range(slots):
                out.append(("S", g, s // NT, s % NT))
                pending.append(("PV", g, s // NT, s % NT))
                if g == 0 and s == lag:
                    out += [("v", i2) for i2 in range(NT // 2)]
                if len(pending) > lag:
                    out.append(pending.pop(0))
                    if out[-1][2:] == (HG - 1, NT - 1):
                        out.append(("ote", out[-1][1]))
                upto = (s - 3) * len(extras) // (slots - 4) if s > 3 else 0
                if s == slots - 1:
                    upto = len(extras)
                out += extras[taken:max(taken, upto)]
                taken = max(taken, upto)
        while pending:
            out.append(pending.pop(0))
        out.append(("ote", G - 1))
        return out

    seq = {-1: tokens() + prep(4), B: outputs()}
    for b in range(B):
        seq[b] = body(b)
    return seq


AUX_DVE = ("zt", "v", "gate", "mx", "mt", "ot", "op")
AUX_ACT = ("q", "k", "at")


def attention(nc, x_sb, ident, w, banded, scratch):
    seq = attention_schedule(banded)
    classes = {
        "aux": AUX_DVE + AUX_ACT, "aux_dve": AUX_DVE, "aux_act": AUX_ACT, "S": ("S",), "PV": ("PV",),
        "ote": ("ote",), "z": ("z",), "mred": ("mred",), "gmul": ("gmul",), "tanh": ("gate",), "qkb": ("q", "k"), "ot": ("ot",),
    }
    done = {c: {} for c in classes}
    slot_user = []
    for c, kinds in classes.items():
        n = 0
        for b in sorted(seq):
            for step in seq[b]:
                if step[0] in kinds and not (c == "qkb" and step[2] == 0):
                    n += 1
                    done[c][b, step] = n
    for b in sorted(seq):
        for step in seq[b]:
            if step[0] in classes["aux"]:
                slot_user.append("aux_dve" if step[0] in AUX_DVE else "aux_act")

    def count(c, step, back=0, minus=0):
        def of(b):
            n = done[c].get((b - back, step))
            return None if n is None or n - minus <= 0 else n - minus
        return of

    def slot_free(step):
        def of(b):
            n = done["aux"][b, step] - 3
            return None if n < 0 else slot_user[:n + 1].count(slot_user[n])
        def who(b):
            n = done["aux"][b, step] - 3
            return None if n < 0 else slot_user[n]
        return who, of

    def bank(b, step):
        b = 1 if not isinstance(b, int) else b
        return (done["aux"][b, step] - 1) % 2

    NP = 2 if banded else 4
    PW = SPAN if banded else N
    col = {}
    if banded:
        wq_cols = lambda m, kd: w["qkv"][kd * P:(kd + 1) * P, m * D:(m + 1) * D].rearrange("p (h d) -> p h d", d=HD)
        bias_of = lambda m: w["bqkv"][m * D:(m + 1) * D].rearrange("(h d) -> h d", d=HD)
    else:
        wq_cols = lambda m, kd: w["qkv"][kd * P:(kd + 1) * P, :].rearrange("p (h m d) -> p h m d", m=3, d=HD)[:, :, m, :]
        bias_of = lambda m: w["bqkv"].rearrange("(h m d) -> h m d", m=3, d=HD)[:, m, :]

    with ExitStack() as ctx:
        tag = "a_" if banded else "b_"
        sb = lambda name, shape, dt=F32: ctx.enter_context(nc.sbuf_tensor(tag + name, shape, dt))
        sem = lambda name: ctx.enter_context(nc.semaphore(tag + name))

        wqk = sb("wqk", [P, 2, KD, G, HG, 32])
        wv = sb("wv", [P, KD, H, HD])
        wout = sb("wout", [P, KD, D])
        bqk = sb("bqk", [P, 2, G])
        row16 = sb("row16", [P, HG])
        bv = sb("bv", [P, D])
        bout = sb("bout", [1, D])
        ones_row = sb("ones_row", [1, P])
        mv = sb("mv", [P, B * NT, 2])
        rstd = sb("rstd", [P, B * NT])
        if banded:
            wgate = sb("wgate", [P, KD, D])
            bgate = sb("bgate", [P, D])
            bias_k = sb("bias_k", [P, H, SPAN])
            bias_q = sb("bias_q", [P, H, SPAN], BF16)
            gate = sb("gate", [P, NT, D])
        else:
            causal = sb("causal", [P, SPAN])

        with ExitStack() as setup:
            ssb = lambda name, shape, dt=F32: setup.enter_context(nc.sbuf_tensor(tag + name, shape, dt))
            ssem = lambda name: setup.enter_context(nc.semaphore(tag + name))
            stats = ssb("stats", [P, B * NT, 6])
            std = ssb("std", [P, B * NT])
            is_row16 = ssb("is_row16", [P, 1])
            gaps_zero, weights_in, stat_steps, std_ready = (ssem(n) for n in ("gaps_zero", "weights_in", "stat_steps", "std_ready"))
            pool_steps, small_steps, lines_out, bias_in, pos_in = (ssem(n) for n in ("pool_steps", "small_steps", "lines_out", "bias_in", "pos_in"))
            if banded:
                pos = ssb("pos", [H, len(OFFSETS)])
                line_k = ssb("line_k", [H, LINE])
                line_q = ssb("line_q", [H, LINE], BF16)
            n_loads = 2 * KD + (KD if not banded else 1) + 1 + 2 * HG + 1 + 1 + (2 if banded else 0)
            with nc.Block() as block:
                @block.sync
                def _(sp):
                    sp.wait_ge(gaps_zero, 2)
                    with nc.allow_non_contiguous_dma(reason="heads' weights and biases, loaded once"):
                        for m in range(2):
                            for kd in range(KD):
                                sp.dma_start(wqk[:, m, kd, :, :, 0:HD].rearrange("p g h d -> p (g h) d"),
                                             wq_cols(m, kd)).then_inc(weights_in, 16)
                            for h in range(HG):
                                sp.dma_start(bqk[32 * h:32 * h + HD, m, :],
                                             bias_of(m).rearrange("(g h) d -> d h g", h=HG)[:, h, :]).then_inc(weights_in, 16)
                        if banded:
                            sp.dma_start(wv[:, :, :, :].rearrange("p k h d -> p k (h d)"),
                                         w["qkv"][:, 2 * D:3 * D].rearrange("(k p) n -> p k n", p=P)).then_inc(weights_in, 16)
                        else:
                            for kd in range(KD):
                                sp.dma_start(wv[:, kd, :, :], wq_cols(2, kd)).then_inc(weights_in, 16)
                        sp.dma_start(bv[:, :].rearrange("p (h d) -> p h d", d=HD),
                                     bass.AP(bias_of(2).tensor, bias_of(2).offset, [[0, P]] + [list(a) for a in bias_of(2).ap])
                                     ).then_inc(weights_in, 16)
                    sp.dma_start(wout[:, :, :], w["out"].rearrange("(k p) n -> p k n", p=P)).then_inc(weights_in, 16)
                    sp.dma_start(bout[:, :], w["bout"].rearrange("(a n) -> a n", a=1)).then_inc(weights_in, 16)
                    if banded:
                        sp.dma_start(wgate[:, :, :], w["gate"].rearrange("(k p) n -> p k n", p=P)).then_inc(weights_in, 16)
                        sp.dma_start(bgate[:, :], bass.AP(w["bgate"].tensor, 0, [[0, P], [1, D]])).then_inc(weights_in, 16)
                    sp.wait_ge(weights_in, 16 * n_loads)

                @block.gpsimd
                def _(pool):
                    pool.memset(wqk[:, :, :, :, :, :], 0.0).then_inc(gaps_zero, 1)
                    pool.memset(bqk[:, :, :], 0.0).then_inc(gaps_zero, 1)
                    pool.memset(row16[:, :], 0.0).then_inc(pool_steps, 1)
                    pool.memset(ones_row[:, :], 1.0).then_inc(pool_steps, 1)
                    pool.wait_ge(pool_steps, 2)
                    pool.affine_select(out=row16[:, :], in_=row16[:, :], compare_op=ALU.not_equal, fill=1.0, base=-HD,
                                       pattern=[[-32, HG]], channel_multiplier=1).then_inc(pool_steps, 1)
                    if not banded:
                        pool.memset(causal[:, :], 0.0).then_inc(pool_steps, 1)
                        pool.wait_ge(pool_steps, 4)
                        last = causal[:, SPAN - P:SPAN]
                        pool.affine_select(out=last, in_=last, compare_op=ALU.is_ge, fill=NEG, base=0,
                                           pattern=[[-1, P]], channel_multiplier=1).then_inc(pool_steps, 1)

                @block.scalar
                def _(act):
                    if banded:
                        with nc.allow_non_contiguous_dma(reason="640 biases, transposed"):
                            act.dma_start(pos[:, :], w["pos_bias"].rearrange("o h -> h o")).then_inc(pos_in, 16)
                        act.wait_ge(small_steps, 2 + 2 * len(OFFSETS))
                        act.dma_start(scratch["line_k"].ap(), line_k[:, :].unsqueeze(1).to_broadcast([H, P, LINE])).then_inc(lines_out, 16)
                        act.dma_start(scratch["line_q"].ap(), line_q[:, :].unsqueeze(1).to_broadcast([H, P, LINE])).then_inc(lines_out, 16)
                        act.wait_ge(lines_out, 32)
                        for h in range(H):
                            act.dma_start(bias_k[:, h, :], window(scratch["line_k"].ap(), h)).then_inc(bias_in, 16)
                            act.dma_start(bias_q[:, h, :], window(scratch["line_q"].ap(), h)).then_inc(bias_in, 16)
                    act.wait_ge(stat_steps, STATS_STEPS)
                    act.activation(std[:, :], std[:, :], ACT.Sqrt).then_inc(std_ready, 1)
                    if banded:
                        act.wait_ge(bias_in, 2 * 16 * H)

                @block.vector
                def _(dve):
                    if banded:
                        dve.memset(line_k[:, :], NEG).then_inc(small_steps, 1)
                        dve.memset(line_q[:, :], NEG).then_inc(small_steps, 1)
                        dve.wait_ge(small_steps, 2)
                        dve.wait_ge(pos_in, 16)
                        for n, off in enumerate(OFFSETS):
                            k, q = off + P - 1, SPAN - 1 - off
                            dve.tensor_copy(line_k[:, k:k + 1], pos[:, n:n + 1]).then_inc(small_steps, 1)
                            dve.tensor_copy(line_q[:, q:q + 1], pos[:, n:n + 1]).then_inc(small_steps, 1)
                    layer_norm_stats(dve, std_ready, stat_steps, x_sb, stats, mv, std, rstd)
                    dve.wait_ge(weights_in, 16 * n_loads)
                    dve.wait_ge(pool_steps, 3)
                    dve.tensor_reduce(is_row16[:, :], row16[:, :], AX.X, ALU.add).then_inc(stat_steps, 1)
                    dve.wait_ge(stat_steps, STATS_STEPS + 2)
                    dve.tensor_scalar(bqk[:, 1, :], bqk[:, 1, :], is_row16[:, :], None, ALU.add).then_inc(stat_steps, 1)
                    dve.tensor_scalar(bqk[:, 0, :], bqk[:, 0, :], HD ** -0.5, None, ALU.mult).then_inc(stat_steps, 1)
                    if banded:
                        dve.tensor_scalar(bout[:, :], bout[:, :], 2.0, None, ALU.mult).then_inc(stat_steps, 1)

        zb = sb("zb", [P, 2, 2, D])
        zT = sb("zT", [P, KD, N])
        qT = [sb(f"qT{n}", [P, N]) for n in range(2)]
        kT = [sb(f"kT{n}", [P, N]) for n in range(2)]
        qT16 = sb("qT16", [P, N], BF16)
        kT16 = sb("kT16", [P, N], BF16)
        v1 = sb("v1", [P, NT, H, HD + 1])
        probs = [sb(f"probs{n}", [P, PW]) for n in range(NP)]
        maxima = sb("maxima", [P, HG, NT, 2])
        neg_max = sb("neg_max", [P, NT, HG, 32])
        outT = sb("outT", [P, N])
        recip = sb("recip", [P, 2, 4, HG])
        flat = sb("flat", [P, NT, D])
        flatT = sb("flatT", [P, 2, 4 * P])

        scoresT_ps = [ctx.enter_context(nc.psum_tensor(f"{tag}scoresT{n}", [P, N], F32)) for n in range(2)]
        outT_ps = ctx.enter_context(nc.psum_tensor(f"{tag}outT_ps", [P, N], F32))
        aux_ps = [ctx.enter_context(nc.psum_tensor(f"{tag}aux{n}", [P, 512], F32)) for n in range(2)]

        cleared = sem("cleared")
        s = {c: sem(c) for c in ("aux", "aux_dve", "aux_act", "S", "PV", "ote", "z", "mred", "gmul", "tanh", "qkb")}
        added = sem("added")
        probs_ready = sem("probs_ready")
        masked = sem("masked")
        passed = sem("passed")
        dve_chain = sem("dve_chain")

        def width(j):
            return min(PW, N - j * P)

        def batches(eng, emit):
            emit(-1)
            emit(0)
            with eng.Fori(1, B - 1) as b:
                emit(b)
            emit(B - 1)
            emit(B)

        def steps(b):
            return seq[b if isinstance(b, int) else 1]

        def nth(b, c, step, minus=0):
            return count(c, step, 0, minus)

        with nc.Block() as block:
            @block.vector
            def _(dve):
                dve.memset(neg_max[:, :, :, :], 0.0).then_inc(cleared, 1)
                dve.memset(maxima[:, :, :, :], LOWEST).then_inc(cleared, 1)
                dve.memset(v1[:, :, :, :], 1.0).then_inc(cleared, 1)
                dve.memset(outT_ps[:, :], 0.0).then_inc(cleared, 1)
                dve.wait_ge(cleared, 4)

                def emit(b):
                    for step in steps(b):
                        kind = step[0]
                        if kind == "S" and banded:
                            _, g, h, j = step
                            n = (h * NT + j) % 2
                            wait(dve, s["S"], b, count("S", step))
                            wait(dve, s["PV"], b, count("S", step, minus=NP))
                            dve.tensor_tensor(probs[n][:, 0:width(j)], scoresT_ps[n][:, 0:width(j)],
                                              bias_k[:, HG * g + h, 0:width(j)], ALU.add).then_inc(added, 1)
                        if kind == "z":
                            i2 = step[1]
                            if i2 >= 2:
                                wait(dve, s["aux"], b, count("aux", ("zt", i2 - 2)))
                            for ii in range(2):
                                tile = (b + 1) * NT + 2 * i2 + ii
                                ins = dve.tensor_scalar(zb[:, i2 % 2, ii, :], x_sb[:, bass.ds(tile, 1), :].rearrange("p a d -> p (a d)"),
                                                        mv[:, bass.ds(tile, 1), 0], rstd[:, bass.ds(tile, 1)],
                                                        ALU.subtract, ALU.mult)
                            ins.then_inc(s["z"], 1)
                        if kind == "mred":
                            g = step[1]
                            last = ("mx", g, HG - 1, NT - 1, 0 if banded else 1)
                            wait(dve, s["aux_dve"], b, count("aux_dve", last))
                            dve.tensor_reduce(neg_max[:, :, :, HD].rearrange("p i h -> p h i"),
                                              maxima[:, :, :, :], AX.X, ALU.max, negate=True).then_inc(s["mred"], 1)
                        if kind == "gmul":
                            wait(dve, s["tanh"], b, count("tanh", ("gate", NT // 2 - 1), back=1))
                            wait(dve, s["aux_dve"], b, count("aux_dve", ("ot", 3, 1)))
                            dve.scalar_tensor_tensor(out=flat[:, :, :], in0=gate[:, :, :], scalar=1.0, in1=flat[:, :, :],
                                                     op0=ALU.add, op1=ALU.mult).then_inc(s["gmul"], 1)
                        if kind not in AUX_DVE:
                            continue
                        src = aux_ps[bank(b, step)]
                        if kind == "mx":
                            wait_alone(dve, s["aux"], b, count("aux", step), passed)
                        else:
                            wait(dve, s["aux"], b, count("aux", step))
                        if kind == "zt":
                            i2 = step[1]
                            ins = dve.tensor_copy(
                                zT[:, :, i2 * 2 * P:(i2 + 1) * 2 * P].rearrange("p k (i q) -> p i k q", q=P),
                                src[:, :].rearrange("p (i k q) -> p i k q", i=2, k=KD))
                        elif kind == "v":
                            for ii in range(2):
                                ins = dve.tensor_tensor(v1[:, 2 * step[1] + ii, :, 0:HD],
                                                        src[:, ii * D:(ii + 1) * D].rearrange("p (h d) -> p h d", d=HD),
                                                        bv[:, :].rearrange("p (h d) -> p h d", d=HD), ALU.add)
                        elif kind == "gate":
                            for ii in range(2):
                                ins = dve.tensor_tensor(gate[:, 2 * step[1] + ii, :], src[:, ii * D:(ii + 1) * D],
                                                        bgate[:, :], ALU.add)
                        elif kind == "mx":
                            _, g, h, i, c = step
                            if banded:
                                wid, mask = min(SPAN, (i + 1) * P), bias_q[:, HG * (g % G) + h, :]
                            else:
                                wid, mask = min(512, (i + 1) * P - 512 * c), causal[:, :]
                            if not banded and i >= 4 and c == 0:
                                ins = dve.tensor_reduce(maxima[:, h, i, c:c + 1], src[:, :], AX.X, ALU.max)
                            else:
                                ins = dve.tensor_tensor_reduce(src[:, 0:wid], src[:, 0:wid], mask[:, SPAN - wid:SPAN],
                                                               1.0, LOWEST, ALU.add, ALU.max, maxima[:, h, i, c:c + 1])
                        elif kind == "mt":
                            _, g, c = step
                            half = qT[g % 2][:, c * 512:(c + 1) * 512]
                            ins = dve.tensor_tensor(half, src[:, :], half, ALU.add)
                        elif kind == "ot":
                            _, g, c = step
                            o = src[:, :].rearrange("p (i h d) -> p i h d", i=4, h=HG)
                            ins = dve.reciprocal(recip[:, c, :, :], o[:, :, :, HD])
                            ins.then_inc(dve_chain, 1)
                            wait(dve, dve_chain, b, count("ot", step))
                            ins = dve.tensor_tensor(
                                flat[:, 4 * c:4 * c + 4, g * HG * HD:(g + 1) * HG * HD].rearrange("p i (h d) -> p i h d", d=HD),
                                o[:, :, :, 0:HD], recip[:, c, :, :].unsqueeze(3).to_broadcast([P, 4, HG, HD]), ALU.mult)
                        elif kind == "op":
                            tile = (b - 1) * NT + 2 * step[1]
                            xt = x_sb[:, bass.ds(tile, 2), :]
                            ins = dve.scalar_tensor_tensor(out=xt, in0=src[:, :].rearrange("p (i d) -> p i d", i=2),
                                                           scalar=0.5 if banded else 1.0, in1=xt, op0=ALU.mult, op1=ALU.add)
                        ins.then_inc(s["aux_dve"], 1)

                batches(dve, emit)

            @block.scalar
            def _(act):
                def emit(b):
                    for step in steps(b):
                        kind = step[0]
                        if kind == "S":
                            _, g, h, j = step
                            n = h * NT + j
                            if banded:
                                wait(act, added, b, count("S", step))
                                src = probs[n % NP][:, 0:width(j)]
                            else:
                                wait(act, s["S"], b, count("S", step))
                                wait(act, s["PV"], b, count("S", step, minus=NP))
                                src = scoresT_ps[n % 2][:, 0:width(j)]
                            act.activation(probs[n % NP][:, 0:width(j)], src, ACT.Exp).then_inc(probs_ready, 1)
                        elif kind == "ote":
                            g = step[1]
                            wait(act, s["PV"], b, count("PV", ("PV", g, HG - 1, NT - 1)))
                            wait(act, s["aux"], b, count("aux", ("ot", (g - 1) % G, 1)))
                            act.activation(outT[:, :], outT_ps[:, :], ACT.Copy).then_inc(s["ote"], 1)
                        elif kind in ("q", "k"):
                            _, g, c = step
                            m = 0 if kind == "q" else 1
                            wait(act, s["aux"], b, count("aux", step))
                            act.activation((qT, kT)[m][g % 2][:, c * 512:(c + 1) * 512], aux_ps[bank(b, step)][:, :], ACT.Identity,
                                           bias=bqk[:, m, g % G:g % G + 1], scale=HD ** -0.5 if m == 0 else 1.0
                                           ).then_inc(s["aux_act"], 1)
                        elif kind == "at":
                            wait(act, s["aux"], b, count("aux", step))
                            act.activation(flatT[:, step[1] % 2, :], aux_ps[bank(b, step)][:, :], ACT.Copy).then_inc(s["aux_act"], 1)
                        elif kind == "gate":
                            i2 = step[1]
                            wait(act, s["aux_dve"], b, count("aux_dve", step))
                            pair = gate[:, 2 * i2:2 * i2 + 2, :]
                            act.activation(pair, pair, ACT.Tanh, scale=0.5).then_inc(s["tanh"], 1)

                batches(act, emit)

            @block.gpsimd
            def _(pool):
                def emit(b):
                    for step in steps(b):
                        kind = step[0]
                        if kind in ("q", "k") and step[2] == 1:
                            g = step[1]
                            wait_alone(pool, s["aux_act"], b, count("aux_act", step), passed)
                            last = ("mx", G if g == 1 else g - 1, HG - 1, NT - 1, 0 if banded else 1)
                            wait_alone(pool, s["aux"], b, count("aux", last, back=1 if g == 1 else 0), passed)
                            full, low = (qT, qT16) if kind == "q" else (kT, kT16)
                            ins = pool.tensor_copy(low[:, :], full[g % 2][:, :])
                            ins.then_inc(s["qkb"], 1)
                        elif kind == "S" and not banded:
                            _, g, h, j = step
                            n = h * NT + j
                            wait_alone(pool, probs_ready, b, count("S", step), passed)
                            tri = probs[n % NP][:, 0:P]
                            pool.affine_select(out=tri, in_=tri, compare_op=ALU.is_ge, fill=0.0, base=0,
                                               pattern=[[1, P]], channel_multiplier=-1).then_inc(masked, 1)

                batches(pool, emit)

            @block.tensor
            def _(pe):
                pe.wait_ge(cleared, 4)

                def free_slot(b, step):
                    who, of = slot_free(step)
                    c = who(b if isinstance(b, int) else 1)
                    if c is None:
                        return
                    assert isinstance(b, int) or who(2) == c
                    wait(pe, s[c], b, of)

                def emit(b):
                    for step in steps(b):
                        kind = step[0]
                        if kind in AUX_DVE + AUX_ACT:
                            free_slot(b, step)
                            dst = aux_ps[bank(b, step)]
                        if kind == "S":
                            _, g, h, j = step
                            n, rows = h * NT + j, slice(32 * h, 32 * h + HD + 1)
                            if h == 0 and j == 0:
                                if g:
                                    wait(pe, s["aux_dve"], b, count("aux_dve", ("mt", g, 1)))
                                else:
                                    wait(pe, s["aux_dve"], b, count("aux_dve", ("mt", G, 1), back=1))
                            wait(pe, added if banded else probs_ready, b, count("S", step, minus=2))
                            for c in range(0, width(j), 512):
                                wid = min(512, width(j) - c)
                                ins = pe.matmul(scoresT_ps[n % 2][:, c:c + wid], kT[g % 2][rows, j * P:(j + 1) * P],
                                                qT[g % 2][rows, j * P + c:j * P + c + wid], start=True, stop=True)
                            ins.then_inc(s["S"], 1)
                        elif kind == "PV":
                            _, g, h, j = step
                            n = h * NT + j
                            like = ("S",) + step[1:]
                            if h == 0 and j == 0:
                                if g:
                                    wait(pe, s["ote"], b, count("ote", ("ote", g - 1)))
                                else:
                                    wait(pe, s["ote"], b, count("ote", ("ote", G - 1), back=1))
                                    wait(pe, s["aux_dve"], b, count("aux_dve", ("v", NT // 2 - 1)))
                            wait(pe, probs_ready if banded else masked, b, count("S", like))
                            lo, hi = j * P, j * P + width(j)
                            while lo < hi:
                                top = min(hi, (lo // 512 + 1) * 512)
                                first = j == (0 if (lo < 512 or not banded) else 1)
                                ins = pe.matmul(outT_ps[32 * h:32 * h + HD + 1, lo:top], v1[:, j, HG * g + h, :],
                                                probs[n % NP][:, lo - j * P:top - j * P], start=first, stop=j == NT - 1,
                                                skip_group_check=True)
                                lo = top
                            ins.then_inc(s["PV"], 1)
                        elif kind == "zt":
                            i2 = step[1]
                            wait(pe, s["z"], b, count("z", ("z", i2)))
                            for ii in range(2):
                                for kd in range(KD):
                                    ins = pe.transpose(dst[:, (ii * KD + kd) * P:(ii * KD + kd + 1) * P],
                                                       zb[:, i2 % 2, ii, kd * P:(kd + 1) * P], ident[:, :])
                            ins.then_inc(s["aux"], 1)
                        elif kind in ("q", "k"):
                            _, g, c = step
                            if g == G:
                                wait(pe, s["aux_dve"], b, count("aux_dve", ("zt", NT // 2 - 1)))
                            for kd in range(KD):
                                ins = pe.matmul(dst[:, :], wqk[:, 0 if kind == "q" else 1, kd, g % G, :, :].rearrange("p h d -> p (h d)"),
                                                zT[:, kd, c * 512:(c + 1) * 512], start=kd == 0, stop=kd == KD - 1)
                            ins.then_inc(s["aux"], 1)
                        elif kind in ("v", "gate"):
                            i2 = step[1]
                            for ii in range(2):
                                tile = slice((2 * i2 + ii) * P, (2 * i2 + ii + 1) * P)
                                for kd in range(KD):
                                    rhs = wv[:, kd, :, :].rearrange("p h d -> p (h d)") if kind == "v" else wgate[:, kd, :]
                                    ins = pe.matmul(dst[:, ii * D:(ii + 1) * D], zT[:, kd, tile], rhs,
                                                    start=kd == 0, stop=kd == KD - 1)
                            ins.then_inc(s["aux"], 1)
                        elif kind == "mx":
                            _, g, h, i, c = step
                            rows = slice(32 * h, 32 * h + HD)
                            if h == 0 and i == 0:
                                wait(pe, s["qkb"], b, count("qkb", ("k", g, 1)))
                            if banded:
                                k0, wid = max(0, (i + 1) * P - SPAN), min(SPAN, (i + 1) * P)
                            else:
                                k0, wid = 512 * c, min(512, (i + 1) * P - 512 * c)
                            pe.matmul(dst[:, 0:wid], qT16[rows, i * P:(i + 1) * P], kT16[rows, k0:k0 + wid],
                                      start=True, stop=True).then_inc(s["aux"], 1)
                        elif kind == "mt":
                            _, g, c = step
                            if c == 0:
                                wait(pe, s["mred"], b, count("mred", ("mred", g)))
                            for i in range(4):
                                ins = pe.transpose(dst[:, i * P:(i + 1) * P],
                                                   neg_max[:, 4 * c + i, :, :].rearrange("p h d -> p (h d)"), ident[:, :])
                            ins.then_inc(s["aux"], 1)
                        elif kind == "ot":
                            _, g, c = step
                            wait(pe, s["ote"], b, count("ote", ("ote", g), back=1 if g == G - 1 else 0))
                            for i in range(4):
                                ins = pe.transpose(dst[:, i * P:(i + 1) * P], outT[:, (4 * c + i) * P:(4 * c + i + 1) * P], ident[:, :])
                            ins.then_inc(s["aux"], 1)
                        elif kind == "at":
                            i2 = step[1]
                            if i2 == 0:
                                if banded:
                                    wait(pe, s["gmul"], b, count("gmul", ("gmul",)))
                                else:
                                    wait(pe, s["aux_dve"], b, count("aux_dve", ("ot", 3, 1)))
                            for ii in range(2):
                                for kd in range(KD):
                                    ins = pe.transpose(dst[:, (ii * KD + kd) * P:(ii * KD + kd + 1) * P],
                                                       flat[:, 2 * i2 + ii, kd * P:(kd + 1) * P], ident[:, :])
                            ins.then_inc(s["aux"], 1)
                        elif kind == "op":
                            i2 = step[1]
                            wait(pe, s["aux_act"], b, count("aux_act", ("at", i2)))
                            for ii in range(2):
                                for kd in range(KD):
                                    pe.matmul(dst[:, ii * D:(ii + 1) * D], flatT[:, i2 % 2, (ii * KD + kd) * P:(ii * KD + kd + 1) * P],
                                              wout[:, kd, :], start=kd == 0, stop=False)
                                ins = pe.matmul(dst[:, ii * D:(ii + 1) * D], ones_row[:, :], bout[:, :], start=False, stop=True)
                            ins.then_inc(s["aux"], 1)

                batches(pe, emit)



SLOTS = 4
QUADS = NE // 4


def ffn(nc, x_sb, ident, w, tag):
    with ExitStack() as ctx:
        sb = lambda name, shape, dt=F32: ctx.enter_context(nc.sbuf_tensor(tag + name, shape, dt))
        sem = lambda name: ctx.enter_context(nc.semaphore(tag + name))
        mv = sb("mv", [P, B * NT, 2])
        rstd = sb("rstd", [P, B * NT])
        gate_wT = sb("gate_wT", [P, KD, NE])
        gate_b = sb("gate_b", [P, 1])
        b1T = sb("b1T", [P, HE // P, NE])
        b2 = sb("b2", [P, D])
        wT = sb("wT", [P, 2, N])
        wtok = sb("wtok", [P, NT, 2, P])
        mergedT = sb("mergedT", [P, KD, NE, B])
        w1_ring = sb("w1_ring", [P, SLOTS, KD, HE])
        w2_ring = sb("w2_ring", [P, SLOTS, HE // P, D])
        w1_in = [sem(f"w1_in{n}") for n in range(SLOTS)]
        w2_in = [sem(f"w2_in{n}") for n in range(SLOTS)]
        o_experts = sb("o_experts", [P, QUADS, D])
        o_batch = sb("o_batch", [P, 2, D])
        bank = [ctx.enter_context(nc.psum_tensor(f"{tag}ps{n}", [P, 512], F32)) for n in range(8)]

        def load_expert(eng, e, n):
            eng.dma_start(w1_ring[:, n, :, :], w["w1"][bass.ds(e, 1), 0:D, :].rearrange("a (p k) h -> p (a k) h", k=KD)
                          ).then_inc(w1_in[n], 16)
            eng.dma_start(w2_ring[:, n, :, :], w["w2"][bass.ds(e, 1), 0:HE, :].rearrange("a (p c) d -> p (a c) d", c=HE // P)
                          ).then_inc(w2_in[n], 16)

        with ExitStack() as setup:
            ssb = lambda name, shape: setup.enter_context(nc.sbuf_tensor(tag + name, shape, F32))
            stats, std = ssb("stats", [P, B * NT, 6]), ssb("std", [P, B * NT])
            b1 = ssb("b1", [NE, HE])
            gw = ssb("gw", [NE, D])
            small_in, stat_steps, std_ready, turned, copied = (
                setup.enter_context(nc.semaphore(tag + n)) for n in ("small_in", "stat_steps", "std_ready", "turned", "copied"))
            with nc.Block() as block:
                @block.sync
                def _(sp):
                    sp.dma_start(b1[:, :], w["w1"][:, D, :]).then_inc(small_in, 16)
                    sp.dma_start(gw[:, :], w["gate_w"]).then_inc(small_in, 16)
                    for q in range(4):
                        sp.dma_start(b2[32 * q:32 * q + NE, :], w["w2"][:, HE, :]).then_inc(small_in, 16)
                        with nc.allow_non_contiguous_dma(reason="32 biases"):
                            sp.dma_start(gate_b[32 * q:32 * q + NE, :], w["gate_b"].rearrange("(e a) -> e a", a=1)).then_inc(small_in, 16)
                    for n in range(SLOTS):
                        load_expert(sp, n, n)

                @block.scalar
                def _(act):
                    act.wait_ge(stat_steps, STATS_STEPS)
                    act.activation(std[:, :], std[:, :], ACT.Sqrt).then_inc(std_ready, 1)

                @block.tensor
                def _(pe):
                    pe.wait_ge(small_in, 160)
                    for c in range(HE // P):
                        pe.transpose(bank[0][:, c * NE:(c + 1) * NE], b1[:, c:HE:HE // P], ident[0:NE, 0:NE])
                    for kd in range(KD):
                        ins = pe.transpose(bank[1][:, kd * NE:(kd + 1) * NE], gw[:, kd * P:(kd + 1) * P], ident[0:NE, 0:NE])
                    ins.then_inc(turned, 1)

                @block.vector
                def _(dve):
                    layer_norm_stats(dve, std_ready, stat_steps, x_sb, stats, mv, std, rstd)
                    dve.wait_ge(turned, 1)
                    dve.tensor_copy(b1T[:, :, :].rearrange("p c e -> p (c e)"), bank[0][:, 0:HE // P * NE]).then_inc(copied, 1)
                    dve.tensor_copy(gate_wT[:, :, :].rearrange("p k e -> p (k e)"), bank[1][:, 0:KD * NE]).then_inc(copied, 1)

        with ExitStack() as choose:
            ssb = lambda name, shape: choose.enter_context(nc.sbuf_tensor(tag + name, shape, F32))
            ssem = lambda name: choose.enter_context(nc.semaphore(tag + name))
            zb = ssb("zb", [P, 4, D])
            zT = ssb("zT", [P, 2, KD, 512])
            logits, marked = ssb("logits", [P, 2, N]), ssb("marked", [P, N])
            top, neg_max, total, inv = (ssb(n, [P, 2, m]) for n, m in (("top", TOPK), ("neg_max", 1), ("total", 1), ("inv", 1)))
            merged = ssb("merged", [P, 2, D])
            z_ready, z_turned, zT_ready, logits_done, logits_ready = (
                ssem(n) for n in ("z_ready", "z_turned", "zT_ready", "logits_done", "logits_ready"))
            top_steps, exp_ready, w_ready, w_turned, wtok_ready = (
                ssem(n) for n in ("top_steps", "exp_ready", "w_ready", "w_turned", "wtok_ready"))
            merge_done, merged_ready, merged_turned = (ssem(n) for n in ("merge_done", "merged_ready", "merged_turned"))
            CH = B * NT // 4
            with nc.Block() as block:
                @block.tensor
                def _(pe):
                    def logit(c):
                        b, half = c // 2, c % 2
                        pe.wait_ge(zT_ready, c + 1)
                        if c >= 2:
                            pe.wait_ge(logits_ready, c - 1)
                        for kd in range(KD):
                            ins = pe.matmul(bank[2 + c % 2][32 * (b % 4):32 * (b % 4) + NE, :], gate_wT[:, kd, :],
                                            zT[:, c % 2, kd, :], start=kd == 0, stop=kd == KD - 1)
                        ins.then_inc(logits_done, 1)

                    for c in range(CH):
                        for ii in range(4):
                            t = 4 * c + ii
                            pe.wait_ge(z_ready, t + 1)
                            if t >= 8 and ii % 2 == 0:
                                pe.wait_ge(zT_ready, (t - 8) // 4 + 1)
                            for kd in range(KD):
                                ins = pe.transpose(bank[(0, 1, 4, 5)[t // 2 % 4]][:, (ii % 2 * KD + kd) * P:(ii % 2 * KD + kd + 1) * P],
                                                   zb[:, t % 4, kd * P:(kd + 1) * P], ident[:, :])
                            ins.then_inc(z_turned, 1)
                        if c:
                            logit(c - 1)
                    logit(CH - 1)
                    for gq in range(2):
                        pe.wait_ge(w_ready, gq + 1)
                        for half in range(2):
                            for ii in range(4):
                                i = 4 * half + ii
                                ins = pe.transpose(bank[4 * gq + half][:, ii * P:(ii + 1) * P], wT[:, gq, i * P:(i + 1) * P], ident[:, :])
                            ins.then_inc(w_turned, 1)
                    for t in range(B * NT):
                        b, i = t // NT, t % NT
                        if t == 0:
                            pe.wait_ge(wtok_ready, 4)
                        pe.wait_ge(z_ready, B * NT + t + 1)
                        q = b % 4
                        pe.matmul(bank[2 + b // 4][32 * q:32 * q + NE, 0:D], wtok[:, i, b // 4, 32 * q:32 * q + NE],
                                  zb[:, t % 4, :], start=i == 0, stop=i == NT - 1).then_inc(merge_done, 1)
                    pe.wait_ge(merged_ready, 2)
                    for gq in range(2):
                        for kd in range(KD):
                            ins = pe.transpose(bank[0][:, (gq * KD + kd) * P:(gq * KD + kd + 1) * P], merged[:, gq, kd:D:KD], ident[:, :])
                    ins.then_inc(merged_turned, 1)

                @block.scalar
                def _(act):
                    for c in range(CH):
                        if c >= 2:
                            act.wait_ge(logits_done, c - 1)
                        for pair in range(2):
                            act.wait_ge(z_turned, 4 * c + 2 * pair + 2)
                            ins = act.activation(
                                zT[:, c % 2, :, 2 * pair * P:2 * (pair + 1) * P].rearrange("p k (i q) -> p i k q", q=P),
                                bank[(0, 1, 4, 5)[(2 * c + pair) % 4]][:, :].rearrange("p (i k q) -> p i k q", i=2, k=KD), ACT.Copy)
                        ins.then_inc(zT_ready, 1)
                    for gq in range(2):
                        act.wait_ge(top_steps, 1 + 3 * gq + 1)
                        act.activation(wT[:, gq, :], logits[:, gq, :], ACT.Exp, bias=neg_max[:, gq, :],
                                       accum_out=total[:, gq, :]).then_inc(exp_ready, 1)
                    for gq in range(2):
                        for half in range(2):
                            act.wait_ge(w_turned, 2 * gq + half + 1)
                            act.activation(wtok[:, 4 * half:4 * half + 4, gq, :],
                                           bank[4 * gq + half][:, :].rearrange("p (i q) -> p i q", q=P), ACT.Copy).then_inc(wtok_ready, 1)

                @block.vector
                def _(dve):
                    def z_tile(t):
                        dve.tensor_scalar(zb[:, t % 4, :], x_sb[:, t, :], mv[:, t, 0:1], rstd[:, t:t + 1],
                                          ALU.subtract, ALU.mult).then_inc(z_ready, 1)

                    def logits_of(c):
                        b, half = c // 2, c % 2
                        rows = slice(32 * (b % 4), 32 * (b % 4) + NE)
                        dve.wait_ge(logits_done, c + 1)
                        dve.tensor_scalar(logits[rows, b // 4, half * 512:(half + 1) * 512], bank[2 + c % 2][rows, :],
                                          gate_b[rows, :], None, ALU.add).then_inc(logits_ready, 1)

                    for c in range(CH):
                        for t in range(4 * c, 4 * c + 4):
                            if t >= 4:
                                dve.wait_ge(z_turned, t - 3)
                            z_tile(t)
                        if c >= 2:
                            logits_of(c - 2)
                    logits_of(CH - 2)
                    logits_of(CH - 1)
                    dve.wait_ge(logits_ready, CH)
                    for gq in range(2):
                        dve.max(top[:, gq, :], logits[:, gq, :]).then_inc(top_steps, 1)
                        dve.wait_ge(top_steps, 3 * gq + 1)
                        dve.tensor_scalar(neg_max[:, gq, :], top[:, gq, 0:1], -1.0, None, ALU.mult).then_inc(top_steps, 1)
                        if gq:
                            dve.wait_ge(w_ready, gq)
                        dve.match_replace(marked[:, :], top[:, gq, :], logits[:, gq, :], LOWEST).then_inc(top_steps, 1)
                        dve.wait_ge(exp_ready, gq + 1)
                        dve.wait_ge(top_steps, 3 * gq + 3)
                        dve.reciprocal(inv[:, gq, :], total[:, gq, :]).then_inc(logits_ready, 1)
                        dve.scalar_tensor_tensor(out=wT[:, gq, :], in0=marked[:, :], scalar=LOWEST, in1=wT[:, gq, :],
                                                 op0=ALU.is_equal, op1=ALU.mult).then_inc(logits_ready, 1)
                        dve.wait_ge(logits_ready, CH + 2 * gq + 2)
                        dve.tensor_scalar(wT[:, gq, :], wT[:, gq, :], inv[:, gq, :], None, ALU.mult).then_inc(w_ready, 1)
                    for t in range(B * NT):
                        if t >= 4:
                            dve.wait_ge(merge_done, t - 3)
                        z_tile(t)
                    dve.wait_ge(merge_done, B * NT)
                    for gq in range(2):
                        dve.tensor_copy(merged[:, gq, :], bank[2 + gq][:, 0:D]).then_inc(merged_ready, 1)
                    dve.wait_ge(merged_turned, 1)
                    for gq in range(2):
                        for kd in range(KD):
                            c0 = (gq * KD + kd) * P
                            dve.tensor_copy(mergedT[:, kd, :, 4 * gq:4 * gq + 4],
                                            bank[0][:, c0:c0 + P].rearrange("p (b e) -> p e b", e=NE)).then_inc(logits_ready, 1)

        with ExitStack() as run:
            rsb = lambda name, shape: run.enter_context(nc.sbuf_tensor(tag + name, shape, F32))
            rsem = lambda name: run.enter_context(nc.semaphore(tag + name))
            lhs1 = [rsb(f"lhs1_{n}", [P, KD, 4, 32]) for n in range(2)]
            hid = [rsb(f"hid{n}", [P, HE]) for n in range(2)]
            hidT = [rsb(f"hidT{n}", [P, HE // P, 4, 32]) for n in range(2)]
            pre = rsb("pre", [P, HE // P, 4, B])
            cleared, lhs1_ready, hid_done, hid_ready, hid_turned, pre_ready, hidT_ready, out_done, out_ready, moved = (
                rsem(n) for n in ("cleared", "lhs1_ready", "hid_done", "hid_ready", "hid_turned", "pre_ready",
                                  "hidT_ready", "out_done", "out_ready", "moved"))
            scattered, summed, o_ready = (rsem(n) for n in ("scattered", "summed", "o_ready"))

            with nc.Block() as block:
                def pairs(eng, emit):
                    emit(0)
                    with eng.Fori(1, QUADS // 2) as it:
                        emit(it)

                @block.sync
                def _(sp):
                    with sp.Fori(0, QUADS - 1) as q:
                        for j in range(4):
                            sp.wait_ge(out_done, q * 4 + j + 1)
                            load_expert(sp, q * 4 + j + SLOTS, j)
                    sp.wait_ge(out_ready, QUADS)
                    for b in range(B):
                        for j in range(4):
                            r0 = 32 * (b % 4) + j
                            sp.dma_start(o_batch[r0:r0 + NE - 3:4, b // 4, :], o_experts[32 * j + b:32 * j + b + 1, :, :]).then_inc(moved, 16)
                    sp.wait_ge(moved, 16 * 4 * B)

                @block.gpsimd
                def _(pool):
                    for n in range(2):
                        pool.memset(lhs1[n][:, :, :, :], 0.0).then_inc(cleared, 1)
                        pool.memset(hidT[n][:, :, :, :], 0.0).then_inc(cleared, 1)
                    pool.wait_ge(cleared, 4)

                    def emit(it):
                        for half in range(2):
                            wait(pool, hid_done, it, lambda i: 2 * i + half - 1 if 2 * i + half >= 2 else None)
                            pool.tensor_copy(lhs1[half][:, :, :, 0:B],
                                             mergedT[:, :, bass.ds(it * 8 + 4 * half, 4), :]).then_inc(lhs1_ready, 1)
                    pairs(pool, emit)

                @block.tensor
                def _(pe):
                    pe.wait_ge(cleared, 4)

                    def up(it, half):
                        wait(pe, lhs1_ready, it, lambda i: 2 * i + half + 1)
                        wait(pe, hid_ready, it, lambda i: 2 * i + half if 2 * i + half else None)
                        for j in range(4):
                            wait(pe, w1_in[j], it, lambda i: 16 * (2 * i + half + 1))
                            for n in range(2):
                                for kd in range(KD):
                                    ins = pe.matmul(bank[n][32 * j:32 * j + 32, :], lhs1[half][:, kd, j, :],
                                                    w1_ring[:, j, kd, n * 512:(n + 1) * 512], start=kd == 0, stop=kd == KD - 1)
                        ins.then_inc(hid_done, 1)

                    def turn(it, half):
                        wait(pe, hid_ready, it, lambda i: 2 * i + half + 1)
                        wait(pe, pre_ready, it, lambda i: 2 * i + half if 2 * i + half else None)
                        for c in range(HE // P):
                            ins = pe.transpose(bank[2 + c // 4][:, c % 4 * P:(c % 4 + 1) * P], hid[half][:, c:HE:HE // P], ident[:, :])
                        ins.then_inc(hid_turned, 1)

                    def down(it, half):
                        wait(pe, hidT_ready, it, lambda i: 2 * i + half + 1)
                        if half == 0:
                            wait(pe, out_ready, it, lambda i: 2 * i - 1 if i else None)
                        else:
                            wait(pe, out_ready, it, lambda i: 2 * i if i else None)
                        for j in range(4):
                            wait(pe, w2_in[j], it, lambda i: 16 * (2 * i + half + 1))
                            for c in range(HE // P):
                                ins = pe.matmul(bank[4 + half][32 * j:32 * j + 32, 0:D], hidT[half][:, c, j, :],
                                                w2_ring[:, j, c, :], start=c == 0, stop=c == HE // P - 1)
                            ins.then_inc(out_done, 1)

                    def emit(it):
                        for half in range(2):
                            up(it, half)
                            turn(it, half)
                            down(it, half)
                    pairs(pe, emit)

                    pe.wait_ge(o_ready, 1)
                    for t2 in range(B * NT // 2):
                        if t2 >= 2:
                            pe.wait_ge(summed, t2 - 1)
                        for ii in range(2):
                            b, i = (2 * t2 + ii) // NT, (2 * t2 + ii) % NT
                            rows = slice(32 * (b % 4), 32 * (b % 4) + NE)
                            ins = pe.matmul(bank[6 + t2 % 2][:, ii * D:(ii + 1) * D], wT[rows, b // 4, i * P:(i + 1) * P],
                                            o_batch[rows, b // 4, :], start=True, stop=True)
                        ins.then_inc(scattered, 1)

                @block.scalar
                def _(act):
                    def emit(it):
                        for half in range(2):
                            wait(act, hid_done, it, lambda i: 2 * i + half + 1)
                            wait(act, hid_turned, it, lambda i: 2 * i + half - 1 if 2 * i + half >= 2 else None)
                            for n in range(2):
                                ins = act.activation(hid[half][:, n * 512:(n + 1) * 512], bank[n][:, :], ACT.Copy)
                            ins.then_inc(hid_ready, 1)
                            wait(act, pre_ready, it, lambda i: 2 * i + half + 1)
                            wait(act, out_done, it, lambda i: 4 * (2 * i + half - 1) if 2 * i + half >= 2 else None)
                            act.activation(hidT[half][:, :, :, 0:B], pre[:, :, :, :], ACT.Gelu).then_inc(hidT_ready, 1)
                            wait(act, out_done, it, lambda i: 4 * (2 * i + half + 1))
                            act.activation(o_experts[:, bass.ds(2 * it + half, 1), :].rearrange("p a d -> p (a d)"),
                                           bank[4 + half][:, 0:D], ACT.Copy).then_inc(out_ready, 1)
                    pairs(act, emit)

                @block.vector
                def _(dve):
                    def emit(it):
                        for half in range(2):
                            wait(dve, hid_turned, it, lambda i: 2 * i + half + 1)
                            wait(dve, hidT_ready, it, lambda i: 2 * i + half if 2 * i + half else None)
                            for n in range(2):
                                ins = dve.tensor_tensor(
                                    pre[:, 4 * n:4 * n + 4, :, :],
                                    bank[2 + n][:, :].rearrange("p (c j r) -> p c j r", c=4, j=4)[:, :, :, 0:B],
                                    b1T[:, 4 * n:4 * n + 4, bass.ds(it * 8 + 4 * half, 4)].unsqueeze(3).to_broadcast([P, 4, 4, B]), ALU.add)
                            ins.then_inc(pre_ready, 1)
                    pairs(dve, emit)
                    dve.wait_ge(moved, 16 * 4 * B)
                    for gq in range(2):
                        ins = dve.tensor_tensor(o_batch[:, gq, :], o_batch[:, gq, :], b2[:, :], ALU.add)
                    ins.then_inc(o_ready, 1)
                    for t2 in range(B * NT // 2):
                        dve.wait_ge(scattered, t2 + 1)
                        xt = x_sb[:, 2 * t2:2 * t2 + 2, :].rearrange("p i d -> p (i d)")
                        dve.tensor_tensor(xt, bank[6 + t2 % 2][:, :], xt, ALU.add).then_inc(summed, 1)


def store(nc, x_sb, out):
    with nc.semaphore("stored") as stored, nc.Block() as block:
        @block.sync
        def _(sp):
            for b in range(B):
                sp.dma_start(out[b].rearrange("(i p) d -> p i d", p=P), x_sb[:, b * NT:(b + 1) * NT, :]).then_inc(stored, 16)
            sp.wait_ge(stored, 16 * B)


STAGES = ("a", "f", "b", "f2")


def build(nc, a, out):
    scratch = {n: nc.dram_tensor(n + "_dram", [H, P, LINE], dt) for n, dt in (("line_k", F32), ("line_q", BF16))}
    attn_a = {"qkv": a["L0_attn_a_Wqkv"], "bqkv": a["L0_attn_a_bqkv"], "out": a["L0_attn_a_Wout"], "bout": a["L0_attn_a_bout"],
              "gate": a["L0_attn_a_Wgate"], "bgate": a["L0_attn_a_bgate"], "pos_bias": a["L0_attn_a_pos_bias"]}
    attn_b = {"qkv": a["L0_attn_b_W1"], "bqkv": a["L0_attn_b_b1"], "out": a["L0_attn_b_W2"], "bout": a["L0_attn_b_b2"]}
    experts = {"gate_w": a["L0_ffn_gate_w"], "gate_b": a["L0_ffn_gate_b"], "w1": a["L0_ffn_w1"], "w2": a["L0_ffn_w2"]}
    with nc.sbuf_tensor("x_sb", [P, B * NT, D], F32) as x_sb, nc.sbuf_tensor("ident", [P, P], F32) as ident:
        build_constants(nc, ident, a["L0_attn_a_x"], x_sb)
        if "a" in STAGES:
            attention(nc, x_sb, ident, attn_a, True, scratch)
        if "f" in STAGES:
            ffn(nc, x_sb, ident, experts, "f1_")
        if "b" in STAGES:
            attention(nc, x_sb, ident, attn_b, False, scratch)
        if "f2" in STAGES:
            ffn(nc, x_sb, ident, experts, "f2_")
        store(nc, x_sb, out)


_INS = ["L0_attn_a_x", "L0_attn_a_Wqkv", "L0_attn_a_bqkv", "L0_attn_a_Wout", "L0_attn_a_bout", "L0_attn_a_Wgate",
        "L0_attn_a_bgate", "L0_attn_a_pos_bias", "L0_attn_b_W1", "L0_attn_b_b1", "L0_attn_b_W2", "L0_attn_b_b2",
        "L0_ffn_gate_w", "L0_ffn_gate_b", "L0_ffn_w1", "L0_ffn_w2"]


def kernel(**inputs):
    import numpy as _np
    import concourse.bacc as _bacc
    from concourse import mybir as _mybir
    from concourse.bass_utils import run_bass_kernel_spmd as _run

    nc = _bacc.Bacc("TRN2", target_bir_lowering=False, num_devices=1)
    arrays, args = {}, {}
    for name in _INS:
        a = _np.ascontiguousarray(inputs[name])
        arrays[f"in_{name}_dram"] = a
        args[name] = nc.dram_tensor(f"in_{name}_dram", a.shape, _mybir.dt.from_np(a.dtype), kind="ExternalInput").ap()
    out = nc.dram_tensor("out_0_dram", (8, 1024, 256), _mybir.dt.float32, kind="ExternalOutput").ap()
    build(nc, args, out)
    r = _run(nc, [arrays], core_ids=[0])
    return r.results[0]["out_0_dram"]
```

```python
from contextlib import ExitStack

import concourse.bass as bass
from concourse import mybir

P = 128
F32 = mybir.dt.float32
BF16 = mybir.dt.bfloat16
ALU = mybir.AluOpType
ACT = mybir.ActivationFunctionType
AX = mybir.AxisListType

B, N, D = 8, 1024, 256
NT = N // P
KD = D // P
H, HD = 16, 16
G, HG = 4, 4
PARTS = 3
PART_PAIRS = ((0, 0), (0, 1), (1, 0), (0, 2), (2, 0), (1, 1))
QK_ROWS = len(PART_PAIRS) * HD
ALL_ROWS = QK_ROWS + PARTS
NE, HE, TOPK = 32, 1024, 8
EPS = 1e-5
NEG = -1e30
LOWEST = -3e38
OFFSETS = sorted(set(range(33)) | {48, 64, 96, 128, 192, 256, 384})
SPAN = 512
LINE = SPAN + P


def window(ap, h):
    return bass.AP(ap.tensor, h * P * LINE + P - 1, [[LINE - 1, P], [1, SPAN]])


def at_iteration(b, count):
    if isinstance(b, int):
        return count(b)
    first, second = count(1), count(2)
    return b * (second - first) + (first - (second - first))


def wait_alone(eng, sem, b, count, passed):
    wait(eng, sem, b, count)
    if not isinstance(b, int):
        eng.sem_inc(passed, 1)


def wait(eng, sem, b, count):
    value = at_iteration(b, count)
    if isinstance(b, int) and not value:
        return
    eng.wait_ge(sem, value)



def build_constants(nc, ident, x, x_sb):
    with nc.semaphore("x_loaded") as x_loaded, nc.semaphore("ident_steps") as ident_steps, nc.Block() as block:
        @block.sync
        def _(sp):
            for b in range(B):
                sp.dma_start(x_sb[:, b * NT:(b + 1) * NT, :],
                             x[b].rearrange("(i p) d -> p i d", p=P)).then_inc(x_loaded, 16)
            sp.wait_ge(x_loaded, 16 * B)

        @block.gpsimd
        def _(pool):
            pool.memset(ident[:, :], 0.0).then_inc(ident_steps, 1)
            pool.wait_ge(ident_steps, 1)
            pool.affine_select(out=ident[:, :], in_=ident[:, :], compare_op=ALU.not_equal, fill=1.0, base=0,
                               pattern=[[-1, P]], channel_multiplier=1).then_inc(ident_steps, 1)
            pool.wait_ge(ident_steps, 2)


def layer_norm_stats(dve, act_sem, dve_sem, x_sb, stats, mv, std, rstd):
    done = 0
    for t in range(B * NT):
        dve.bn_stats(stats[:, t, :], x_sb[:, t, :]).then_inc(dve_sem, 1)
    done += B * NT
    dve.wait_ge(dve_sem, done)
    for t in range(B * NT):
        dve.bn_aggr(mv[:, t, :], stats[:, t, :]).then_inc(dve_sem, 1)
    done += B * NT
    dve.wait_ge(dve_sem, done)
    dve.tensor_scalar(std[:, :], mv[:, :, 1], EPS, None, ALU.add).then_inc(dve_sem, 1)
    done += 1
    dve.wait_ge(act_sem, 1)
    dve.reciprocal(rstd[:, :], std[:, :]).then_inc(dve_sem, 1)
    return done


STATS_STEPS = 2 * B * NT + 1



def pieces(banded, j):
    return 1 if banded or N - j * P <= 512 else 2


def attention_schedule(banded):
    def projections(g):
        out = []
        for kind in "qk":
            out += [(kind, g, 0), (kind, g, 1), ("split", g, kind), ("spill", g, kind)]
        return out

    def operands(g):
        return ([("bias", g)] if banded else []) + [("stack", g)]

    def row_maxima(g):
        return [("mx", g, h, i, c) for h in range(HG) for i in range(NT)
                for c in range(1 if banded or i < 4 else 2)] + [("mred", g), ("mt", g), ("mrow", g)]

    def tokens():
        out = []
        for i2 in range(NT // 2):
            out += [("z", i2), ("zt", i2)]
        return out

    def outputs():
        out = [("ot", 3, 0), ("ot", 3, 1)] + ([("gmul",)] if banded else [])
        return out + [("at", 0), ("at", 1), ("op", 0), ("at", 2), ("op", 1), ("at", 3), ("op", 2), ("op", 3)]

    def body(b):
        out = []
        pending = []
        slots = HG * NT
        cost = [min(SPAN if banded else N, N - (s // HG) * P) + P for s in range(slots)]
        for g in range(G):
            others = [] if g == 0 else [("ot", g - 1, 0), ("ot", g - 1, 1)]
            if g == 0:
                others += (outputs() if b else []) + projections(2)
            if g == 1 and banded:
                others += [("gate", i2) for i2 in range(NT // 2)]
            if g == TOKENS_IN and b < B - 1:
                others += tokens()
            if g == 2 and b < B - 1:
                others += projections(4)
            maxima = row_maxima(g + 1) if g < G - 1 or b < B - 1 else []
            if maxima:
                out += operands(g + 1)
            streams = [[maxima, 0, MAXIMA_FROM, MAXIMA_TO], [others, 0, 0.1, OTHERS_TO]]
            for s in range(slots):
                out += [("S", g, s % HG, s // HG, c) for c in range(pieces(banded, s // HG))]
                pending.append(("PV", g, s % HG, s // HG))
                if g == 0 and s == 2:
                    out += [("v", i2) for i2 in range(NT // 2)]
                if s % HG == HG - 1 and len(pending) > HG:
                    out += pending[:HG]
                    del pending[:HG]
                    if out[-1][2:] == (HG - 1, NT - 1):
                        out.append(("ote", out[-1][1]))
                share = sum(cost[:s + 1]) / sum(cost)
                for stream in streams:
                    work, taken, start, stop = stream
                    upto = min(len(work), max(taken, int(len(work) * (share - start) / (stop - start)))) if s > HG else 0
                    if s == slots - 1:
                        upto = len(work)
                    out += work[taken:upto]
                    stream[1] = upto
        out += pending
        out.append(("ote", G - 1))
        return out

    seq = {-1: tokens() + projections(4) + operands(4) + row_maxima(4), B: outputs()}
    for b in range(B):
        seq[b] = body(b)
    return seq


TOKENS_IN = 1
MAXIMA_FROM, MAXIMA_TO, OTHERS_TO = 0.1, 0.92, 1.0

AUX_DVE = ("zt", "v", "gate", "mx", "mt", "ot", "op")
AUX_ACT = ("q", "k", "at")


def attention(nc, x_sb, ident, w, banded, scratch):
    seq = attention_schedule(banded)
    classes = {
        "aux": AUX_DVE + AUX_ACT, "aux_dve": AUX_DVE, "aux_act": AUX_ACT, "S": ("S",), "PV": ("PV",),
        "ote": ("ote",), "z": ("z",), "mred": ("mred",), "gmul": ("gmul",), "tanh": ("gate",), "ot": ("ot",), "split": ("split",), "spill": ("spill",), "stack": ("stack",), "mrow": ("mrow",), "bias": ("bias",),
    }
    done = {c: {} for c in classes}
    slot_user = []
    for c, kinds in classes.items():
        n = 0
        for b in sorted(seq):
            for step in seq[b]:
                if step[0] in kinds:
                    n += 1
                    done[c][b, step] = n
    for b in sorted(seq):
        for step in seq[b]:
            if step[0] in classes["aux"]:
                slot_user.append("aux_dve" if step[0] in AUX_DVE else "aux_act")

    def count(c, step, back=0, minus=0, each=1, plus=0):
        def of(b):
            n = done[c].get((b - back, step))
            return None if n is None or n - minus <= 0 else each * (n - minus) + plus
        return of

    def slot_free(step):
        def of(b):
            n = done["aux"][b, step] - 1 - NA
            return None if n < 0 else slot_user[:n + 1].count(slot_user[n])
        def who(b):
            n = done["aux"][b, step] - 1 - NA
            return None if n < 0 else slot_user[n]
        return who, of

    def bank(b, step):
        b = 1 if not isinstance(b, int) else b
        return (done["aux"][b, step] - 1) % NA

    NA, NS = (4, 2) if banded else (3, 3)
    NP = 2 * HG
    PW = SPAN if banded else N
    col = {}
    if banded:
        wq_cols = lambda m, kd: w["qkv"][kd * P:(kd + 1) * P, m * D:(m + 1) * D].rearrange("p (h d) -> p h d", d=HD)
        bias_of = lambda m: w["bqkv"][m * D:(m + 1) * D].rearrange("(h d) -> h d", d=HD)
    else:
        wq_cols = lambda m, kd: w["qkv"][kd * P:(kd + 1) * P, :].rearrange("p (h m d) -> p h m d", m=3, d=HD)[:, :, m, :]
        bias_of = lambda m: w["bqkv"].rearrange("(h m d) -> h m d", m=3, d=HD)[:, m, :]

    with ExitStack() as ctx:
        tag = "a_" if banded else "b_"
        sb = lambda name, shape, dt=F32: ctx.enter_context(nc.sbuf_tensor(tag + name, shape, dt))
        sem = lambda name: ctx.enter_context(nc.semaphore(tag + name))

        wqk = sb("wqk", [P, 2, KD, H, HD])
        wv = sb("wv", [P, KD, H, HD])
        wout = sb("wout", [P, KD, D])
        bqk = sb("bqk", [P, 2, 2])
        ident16 = sb("ident16", [P, P], BF16)
        bv = sb("bv", [P, D])
        bout = sb("bout", [1, D])
        ones_row = sb("ones_row", [1, P])
        mv = sb("mv", [P, B * NT, 2])
        rstd = sb("rstd", [P, B * NT])
        if banded:
            wgate = sb("wgate", [P, KD, D])
            bgate = sb("bgate", [P, D])
            bias_k = [sb(f"bias_k{n}", [P, HG, SPAN]) for n in range(2)]
            bias_q = sb("bias_q", [P, H, SPAN], BF16)
            gate = sb("gate", [P, NT, D])
        else:
            causal = sb("causal", [P, SPAN])

        with ExitStack() as setup:
            ssb = lambda name, shape, dt=F32: setup.enter_context(nc.sbuf_tensor(tag + name, shape, dt))
            ssem = lambda name: setup.enter_context(nc.semaphore(tag + name))
            stats = ssb("stats", [P, B * NT, 6])
            std = ssb("std", [P, B * NT])
            weights_in, stat_steps, std_ready = (ssem(n) for n in ("weights_in", "stat_steps", "std_ready"))
            pool_steps, small_steps, lines_out, bias_in, pos_in = (ssem(n) for n in ("pool_steps", "small_steps", "lines_out", "bias_in", "pos_in"))
            if banded:
                pos = ssb("pos", [H, len(OFFSETS)])
                line_k = ssb("line_k", [H, LINE])
                line_q = ssb("line_q", [H, LINE], BF16)
            n_loads = 2 * KD + (KD if not banded else 1) + 1 + 2 * H + 1 + 1 + (2 if banded else 0)
            with nc.Block() as block:
                @block.sync
                def _(sp):
                    with nc.allow_non_contiguous_dma(reason="heads' weights and biases, loaded once"):
                        for m in range(2):
                            for kd in range(KD):
                                sp.dma_start(wqk[:, m, kd, :, :], wq_cols(m, kd)).then_inc(weights_in, 16)
                            for h in range(H):
                                sp.dma_start(bqk[h % 8 * HD:(h % 8 + 1) * HD, m, h // 8:h // 8 + 1],
                                             bias_of(m)[h:h + 1, :].rearrange("a d -> d a")).then_inc(weights_in, 16)
                        if banded:
                            sp.dma_start(wv[:, :, :, :].rearrange("p k h d -> p k (h d)"),
                                         w["qkv"][:, 2 * D:3 * D].rearrange("(k p) n -> p k n", p=P)).then_inc(weights_in, 16)
                        else:
                            for kd in range(KD):
                                sp.dma_start(wv[:, kd, :, :], wq_cols(2, kd)).then_inc(weights_in, 16)
                        sp.dma_start(bv[:, :].rearrange("p (h d) -> p h d", d=HD),
                                     bass.AP(bias_of(2).tensor, bias_of(2).offset, [[0, P]] + [list(a) for a in bias_of(2).ap])
                                     ).then_inc(weights_in, 16)
                    sp.dma_start(wout[:, :, :], w["out"].rearrange("(k p) n -> p k n", p=P)).then_inc(weights_in, 16)
                    sp.dma_start(bout[:, :], w["bout"].rearrange("(a n) -> a n", a=1)).then_inc(weights_in, 16)
                    if banded:
                        sp.dma_start(wgate[:, :, :], w["gate"].rearrange("(k p) n -> p k n", p=P)).then_inc(weights_in, 16)
                        sp.dma_start(bgate[:, :], bass.AP(w["bgate"].tensor, 0, [[0, P], [1, D]])).then_inc(weights_in, 16)
                    sp.wait_ge(weights_in, 16 * n_loads)

                @block.gpsimd
                def _(pool):
                    pool.memset(ones_row[:, :], 1.0).then_inc(pool_steps, 1)
                    pool.memset(ident16[:, :], 0.0).then_inc(pool_steps, 1)
                    pool.wait_ge(pool_steps, 2)
                    pool.affine_select(out=ident16[:, :], in_=ident16[:, :], compare_op=ALU.not_equal, fill=1.0, base=0,
                                       pattern=[[-1, P]], channel_multiplier=1).then_inc(pool_steps, 1)
                    if not banded:
                        pool.memset(causal[:, :], 0.0).then_inc(pool_steps, 1)
                        pool.wait_ge(pool_steps, 4)
                        last = causal[:, SPAN - P:SPAN]
                        pool.affine_select(out=last, in_=last, compare_op=ALU.is_ge, fill=NEG, base=0,
                                           pattern=[[-1, P]], channel_multiplier=1).then_inc(pool_steps, 1)

                @block.scalar
                def _(act):
                    if banded:
                        with nc.allow_non_contiguous_dma(reason="640 biases, transposed"):
                            act.dma_start(pos[:, :], w["pos_bias"].rearrange("o h -> h o")).then_inc(pos_in, 16)
                        act.wait_ge(small_steps, 2 + 2 * len(OFFSETS))
                        act.dma_start(scratch["line_k"].ap(), line_k[:, :].unsqueeze(1).to_broadcast([H, P, LINE])).then_inc(lines_out, 16)
                        act.dma_start(scratch["line_q"].ap(), line_q[:, :].unsqueeze(1).to_broadcast([H, P, LINE])).then_inc(lines_out, 16)
                        act.wait_ge(lines_out, 32)
                        for h in range(H):
                            act.dma_start(bias_q[:, h, :], window(scratch["line_q"].ap(), h)).then_inc(bias_in, 16)
                    act.wait_ge(stat_steps, STATS_STEPS)
                    act.activation(std[:, :], std[:, :], ACT.Sqrt).then_inc(std_ready, 1)
                    if banded:
                        act.wait_ge(bias_in, 16 * H)

                @block.vector
                def _(dve):
                    if banded:
                        dve.memset(line_k[:, :], NEG).then_inc(small_steps, 1)
                        dve.memset(line_q[:, :], NEG).then_inc(small_steps, 1)
                        dve.wait_ge(small_steps, 2)
                        dve.wait_ge(pos_in, 16)
                        for n, off in enumerate(OFFSETS):
                            k, q = off + P - 1, SPAN - 1 - off
                            dve.tensor_copy(line_k[:, k:k + 1], pos[:, n:n + 1]).then_inc(small_steps, 1)
                            dve.tensor_copy(line_q[:, q:q + 1], pos[:, n:n + 1]).then_inc(small_steps, 1)
                    layer_norm_stats(dve, std_ready, stat_steps, x_sb, stats, mv, std, rstd)
                    dve.wait_ge(weights_in, 16 * n_loads)
                    dve.tensor_scalar(bqk[:, 0, :], bqk[:, 0, :], HD ** -0.5, None, ALU.mult).then_inc(stat_steps, 1)
                    if banded:
                        dve.tensor_scalar(bout[:, :], bout[:, :], 2.0, None, ALU.mult).then_inc(stat_steps, 1)

        zb = sb("zb", [P, 2, 2, D])
        zT = sb("zT", [P, KD, N])
        full = sb("full", [P, N])
        parts = [sb(f"parts{n}", [P, PARTS, N], BF16) for n in range(2)]
        q_stack = [sb(f"q_stack{n}", [ALL_ROWS, HG, N], BF16) for n in range(2)]
        k_stack = [sb(f"k_stack{n}", [ALL_ROWS, HG, N], BF16) for n in range(2)]
        v1 = sb("v1", [P, NT, H, HD + 1])
        probs = [sb(f"probs{n}", [P, PW]) for n in range(NP)]
        maxima = sb("maxima", [P, HG, NT, 2])
        neg_max = sb("neg_max", [P, HG, NT])
        neg_max_parts = sb("neg_max_parts", [P, PARTS, HG, NT], BF16)
        neg_max_rows = sb("neg_max_rows", [PARTS * HG * NT, P], BF16)
        outT = sb("outT", [P, N])
        recip = sb("recip", [P, 2, 4, HG])
        flat = sb("flat", [P, NT, D])
        flatT = sb("flatT", [P, 2, 4 * P])

        scoresT_ps = [ctx.enter_context(nc.psum_tensor(f"{tag}scoresT{n}", [P, 512], F32)) for n in range(NS)]
        outT_ps = ctx.enter_context(nc.psum_tensor(f"{tag}outT_ps", [P, N], F32))
        aux_ps = [ctx.enter_context(nc.psum_tensor(f"{tag}aux{n}", [P, 512], F32)) for n in range(NA)]

        cleared = sem("cleared")
        s = {c: sem(c) for c in ("aux", "aux_dve", "aux_act", "S", "PV", "ote", "z", "mred", "gmul", "tanh", "split")}
        spilled, stacked, mrows_in, bias_in = (sem(n) for n in ("spilled", "stacked", "mrows_in", "bias_in"))
        SPILL, STACK, MROW, BIAS = 16 * PARTS, 2 * 16 * len(PART_PAIRS), 16 * PARTS, 16 * HG
        split_chain, mred_chain = sem("split_chain"), sem("mred_chain")
        added = sem("added")
        probs_ready = sem("probs_ready")
        masked = sem("masked")
        passed = sem("passed")
        dve_chain = sem("dve_chain")

        def width(j):
            return min(PW, N - j * P)

        def piece(b, step):
            _, g, h, j, c = step
            b = b if isinstance(b, int) else 1
            return scoresT_ps[(done["S"][b, step] - 1) % NS], 512 * c, min(512, width(j) - 512 * c)

        def batches(eng, emit):
            emit(-1)
            emit(0)
            with eng.Fori(1, B - 1) as b:
                emit(b)
            emit(B - 1)
            emit(B)

        def steps(b):
            return seq[b if isinstance(b, int) else 1]

        def nth(b, c, step, minus=0):
            return count(c, step, 0, minus)

        with nc.Block() as block:
            @block.vector
            def _(dve):
                for n in range(2):
                    dve.memset(k_stack[n][QK_ROWS:ALL_ROWS, :, :], 1.0).then_inc(cleared, 1)
                dve.memset(maxima[:, :, :, :], LOWEST).then_inc(cleared, 1)
                dve.memset(v1[:, :, :, :], 1.0).then_inc(cleared, 1)
                dve.memset(outT_ps[:, :], 0.0).then_inc(cleared, 1)
                dve.wait_ge(cleared, 5)

                def emit(b):
                    for step in steps(b):
                        kind = step[0]
                        if kind == "S" and banded:
                            _, g, h, j, _ = step
                            n = j * HG + h
                            if n == 0:
                                wait(dve, bias_in, b, count("bias", ("bias", g or G), back=0 if g else 1, each=BIAS))
                            wait(dve, s["S"], b, count("S", step))
                            wait(dve, s["PV"], b, count("PV", ("PV", g, h, j), minus=NP))
                            dve.tensor_tensor(probs[n % NP][:, 0:width(j)], piece(b, step)[0][:, 0:width(j)],
                                              bias_k[g % 2][:, h, 0:width(j)], ALU.add).then_inc(added, 1)
                        if kind == "z":
                            i2 = step[1]
                            if i2 >= 2:
                                wait(dve, s["aux"], b, count("aux", ("zt", i2 - 2)))
                            for ii in range(2):
                                tile = (b + 1) * NT + 2 * i2 + ii
                                ins = dve.tensor_scalar(zb[:, i2 % 2, ii, :], x_sb[:, bass.ds(tile, 1), :].rearrange("p a d -> p (a d)"),
                                                        mv[:, bass.ds(tile, 1), 0], rstd[:, bass.ds(tile, 1)],
                                                        ALU.subtract, ALU.mult)
                            ins.then_inc(s["z"], 1)
                        if kind == "mred":
                            g = step[1]
                            last = ("mx", g, HG - 1, NT - 1, 0 if banded else 1)
                            wait(dve, s["aux_dve"], b, count("aux_dve", last))
                            wait(dve, s["aux"], b, count("aux", ("mt", G if g == 1 else g - 1), back=1 if g == 1 else 0))

                            def chained(ins, n):
                                ins.then_inc(mred_chain, 1)
                                wait(dve, mred_chain, b, count("mred", step, each=4, plus=n - 4))
                            part = lambda n: neg_max_parts[:, n, :, :]
                            chained(dve.tensor_reduce(neg_max[:, :, :], maxima[:, :, :, :], AX.X, ALU.max, negate=True), 1)
                            chained(dve.tensor_copy(part(0), neg_max[:, :, :]), 2)
                            chained(dve.tensor_tensor(neg_max[:, :, :], neg_max[:, :, :], part(0), ALU.subtract), 3)
                            chained(dve.tensor_copy(part(1), neg_max[:, :, :]), 4)
                            dve.tensor_tensor(part(2), neg_max[:, :, :], part(1), ALU.subtract).then_inc(s["mred"], 1)
                        if kind == "split":
                            _, g, which = step
                            m = "qk".index(which)
                            wait(dve, s["aux_act"], b, count("aux_act", (which, g, 1)))
                            wait(dve, spilled, b, count("spill", ("spill", 4 if g == 2 else 2, which), back=1 if g == 2 else 0, each=SPILL))

                            def link(ins, n):
                                ins.then_inc(split_chain, 1)
                                wait(dve, split_chain, b, count("split", step, each=3, plus=n - 3))
                            part = lambda n: parts[m][:, n, :]
                            link(dve.tensor_copy(part(0), full[:, :]), 1)
                            link(dve.tensor_tensor(full[:, :], full[:, :], part(0), ALU.subtract), 2)
                            link(dve.tensor_copy(part(1), full[:, :]), 3)
                            dve.tensor_tensor(part(2), full[:, :], part(1), ALU.subtract).then_inc(s["split"], 1)
                        if kind == "gmul":
                            wait(dve, s["tanh"], b, count("tanh", ("gate", NT // 2 - 1), back=1))
                            wait(dve, s["aux_dve"], b, count("aux_dve", ("ot", 3, 1)))
                            dve.scalar_tensor_tensor(out=flat[:, :, :], in0=gate[:, :, :], scalar=1.0, in1=flat[:, :, :],
                                                     op0=ALU.add, op1=ALU.mult).then_inc(s["gmul"], 1)
                        if kind not in AUX_DVE:
                            continue
                        src = aux_ps[bank(b, step)]
                        if kind == "mx":
                            wait_alone(dve, s["aux"], b, count("aux", step), passed)
                        else:
                            wait(dve, s["aux"], b, count("aux", step))
                        if kind == "zt":
                            i2 = step[1]
                            ins = dve.tensor_copy(
                                zT[:, :, i2 * 2 * P:(i2 + 1) * 2 * P].rearrange("p k (i q) -> p i k q", q=P),
                                src[:, :].rearrange("p (i k q) -> p i k q", i=2, k=KD))
                        elif kind == "v":
                            for ii in range(2):
                                ins = dve.tensor_tensor(v1[:, 2 * step[1] + ii, :, 0:HD],
                                                        src[:, ii * D:(ii + 1) * D].rearrange("p (h d) -> p h d", d=HD),
                                                        bv[:, :].rearrange("p (h d) -> p h d", d=HD), ALU.add)
                        elif kind == "gate":
                            for ii in range(2):
                                ins = dve.tensor_tensor(gate[:, 2 * step[1] + ii, :], src[:, ii * D:(ii + 1) * D],
                                                        bgate[:, :], ALU.add)
                        elif kind == "mx":
                            _, g, h, i, c = step
                            if banded:
                                wid, mask = min(SPAN, (i + 1) * P), bias_q[:, HG * (g % G) + h, :]
                            else:
                                wid, mask = min(512, (i + 1) * P - 512 * c), causal[:, :]
                            if not banded and i >= 4 and c == 0:
                                ins = dve.tensor_reduce(maxima[:, h, i, c:c + 1], src[:, :], AX.X, ALU.max)
                            else:
                                ins = dve.tensor_tensor_reduce(src[:, 0:wid], src[:, 0:wid], mask[:, SPAN - wid:SPAN],
                                                               1.0, LOWEST, ALU.add, ALU.max, maxima[:, h, i, c:c + 1])
                        elif kind == "mt":
                            g = step[1]
                            wait(dve, mrows_in, b, count("mrow", ("mrow", G if g == 1 else g - 1), back=1 if g == 1 else 0, each=MROW))
                            ins = dve.tensor_copy(neg_max_rows[:, :], src[:, :].bitcast(BF16)[0:PARTS * HG * NT, 0:P])
                        elif kind == "ot":
                            _, g, c = step
                            o = src[:, :].rearrange("p (i h d) -> p i h d", i=4, h=HG)
                            ins = dve.reciprocal(recip[:, c, :, :], o[:, :, :, HD])
                            ins.then_inc(dve_chain, 1)
                            wait(dve, dve_chain, b, count("ot", step))
                            ins = dve.tensor_tensor(
                                flat[:, 4 * c:4 * c + 4, g * HG * HD:(g + 1) * HG * HD].rearrange("p i (h d) -> p i h d", d=HD),
                                o[:, :, :, 0:HD], recip[:, c, :, :].unsqueeze(3).to_broadcast([P, 4, HG, HD]), ALU.mult)
                        elif kind == "op":
                            tile = (b - 1) * NT + 2 * step[1]
                            xt = x_sb[:, bass.ds(tile, 2), :]
                            ins = dve.scalar_tensor_tensor(out=xt, in0=src[:, :].rearrange("p (i d) -> p i d", i=2),
                                                           scalar=0.5 if banded else 1.0, in1=xt, op0=ALU.mult, op1=ALU.add)
                        ins.then_inc(s["aux_dve"], 1)

                batches(dve, emit)

            @block.scalar
            def _(act):
                def emit(b):
                    for step in steps(b):
                        kind = step[0]
                        if kind == "S":
                            _, g, h, j, c = step
                            n = j * HG + h
                            src, lo, wid = piece(b, step)
                            dst = probs[n % NP][:, lo:lo + wid]
                            if banded:
                                wait(act, added, b, count("S", step))
                                src = dst
                            else:
                                wait(act, s["S"], b, count("S", step))
                                if c == 0:
                                    wait(act, s["PV"], b, count("PV", ("PV", g, h, j), minus=NP))
                                src = src[:, 0:wid]
                            act.activation(dst, src, ACT.Exp).then_inc(probs_ready, 1)
                        elif kind == "ote":
                            g = step[1]
                            wait(act, s["PV"], b, count("PV", ("PV", g, HG - 1, NT - 1)))
                            wait(act, s["aux"], b, count("aux", ("ot", (g - 1) % G, 1)))
                            act.activation(outT[:, :], outT_ps[:, :], ACT.Copy).then_inc(s["ote"], 1)
                        elif kind in ("q", "k"):
                            _, g, c = step
                            m = 0 if kind == "q" else 1
                            wait(act, s["aux"], b, count("aux", step))
                            if c == 0:
                                before = ("split", g, "q") if kind == "k" else ("split", 4 if g == 2 else 2, "k")
                                wait(act, s["split"], b, count("split", before, back=1 if before[1] == 4 and g == 2 else 0))
                            act.activation(full[:, c * 512:(c + 1) * 512], aux_ps[bank(b, step)][:, :], ACT.Identity,
                                           bias=bqk[:, m, g // 2 % 2:g // 2 % 2 + 1], scale=HD ** -0.5 if m == 0 else 1.0
                                           ).then_inc(s["aux_act"], 1)
                        elif kind == "at":
                            wait(act, s["aux"], b, count("aux", step))
                            act.activation(flatT[:, step[1] % 2, :], aux_ps[bank(b, step)][:, :], ACT.Copy).then_inc(s["aux_act"], 1)
                        elif kind == "gate":
                            i2 = step[1]
                            wait(act, s["aux_dve"], b, count("aux_dve", step))
                            pair = gate[:, 2 * i2:2 * i2 + 2, :]
                            act.activation(pair, pair, ACT.Tanh, scale=0.5).then_inc(s["tanh"], 1)

                batches(act, emit)

            @block.gpsimd
            def _(pool):
                def emit(b):
                    for step in steps(b):
                        kind = step[0]
                        if kind == "S" and not banded and step[4] == 0:
                            _, g, h, j, _ = step
                            n = j * HG + h
                            wait_alone(pool, probs_ready, b, count("S", step), passed)
                            tri = probs[n % NP][:, 0:P]
                            pool.affine_select(out=tri, in_=tri, compare_op=ALU.is_ge, fill=0.0, base=0,
                                               pattern=[[1, P]], channel_multiplier=-1).then_inc(masked, 1)

                batches(pool, emit)

            @block.sync
            def _(sp):
                def emit(b):
                    for step in steps(b):
                        kind = step[0]
                        if kind == "bias":
                            g = step[1]
                            last = ("S", (g - 2) % G, HG - 1, NT - 1, 0)
                            wait_alone(sp, added, b, count("S", last, back=1 if g == 1 else 0), passed)
                            for h in range(HG):
                                sp.dma_start(bias_k[g % 2][:, h, :], window(scratch["line_k"].ap(), HG * (g % G) + h)).then_inc(bias_in, 16)
                        elif kind == "spill":
                            _, g, which = step
                            wait_alone(sp, s["split"], b, count("split", ("split", g, which)), passed)
                            wait_alone(sp, stacked, b, count("stack", ("stack", 3 if g == 2 else 1), back=1 if g == 2 else 0, each=STACK), passed)
                            m = "qk".index(which)
                            for part in range(PARTS):
                                sp.dma_start(scratch["parts"].ap()[m, g // 2 % 2, part], parts[m][:, part, :]).then_inc(spilled, 16)
                        elif kind == "stack":
                            g = step[1]
                            even = g - g % 2
                            if even:
                                wait_alone(sp, spilled, b, count("spill", ("spill", even, "k"), each=SPILL), passed)
                            else:
                                wait_alone(sp, spilled, b, count("spill", ("spill", G, "k"), back=1, each=SPILL), passed)
                            last = ("S", (g - 2) % G, HG - 1, NT - 1, 0)
                            wait_alone(sp, s["S"], b, count("S", last, back=1 if g == 1 else 0), passed)
                            for which, stack in enumerate((q_stack, k_stack)):
                                for r, pair in enumerate(PART_PAIRS):
                                    src = scratch["parts"].ap()[which, g // 2 % 2, pair[which], g % 2 * HG * HD:(g % 2 + 1) * HG * HD, :]
                                    sp.dma_start(stack[g % 2][r * HD:(r + 1) * HD, :, :],
                                                 src.rearrange("(h d) n -> d h n", d=HD)).then_inc(stacked, 16)
                        elif kind == "mrow":
                            g = step[1]
                            wait_alone(sp, s["aux_dve"], b, count("aux_dve", ("mt", g)), passed)
                            for part in range(PARTS):
                                sp.dma_start(q_stack[g % 2][QK_ROWS + part:QK_ROWS + part + 1, :, :],
                                             neg_max_rows[part * HG * NT:(part + 1) * HG * NT, :]).then_inc(mrows_in, 16)

                batches(sp, emit)

            @block.tensor
            def _(pe):
                pe.wait_ge(cleared, 5)

                def free_slot(b, step):
                    who, of = slot_free(step)
                    c = who(b if isinstance(b, int) else 1)
                    if c is None:
                        return
                    assert isinstance(b, int) or who(2) == c
                    wait(pe, s[c], b, of)

                def emit(b):
                    for step in steps(b):
                        kind = step[0]
                        if kind in AUX_DVE + AUX_ACT:
                            free_slot(b, step)
                            dst = aux_ps[bank(b, step)]
                        if kind == "S":
                            _, g, h, j, _ = step
                            n = j * HG + h
                            if n == 0:
                                wait(pe, mrows_in, b, count("mrow", ("mrow", g or G), back=0 if g else 1, each=MROW))
                            wait(pe, added if banded else probs_ready, b, count("S", step, minus=NS))
                            dst, lo, wid = piece(b, step)
                            pe.matmul(dst[:, 0:wid], k_stack[g % 2][:, h, j * P:(j + 1) * P],
                                      q_stack[g % 2][:, h, j * P + lo:j * P + lo + wid], start=True, stop=True).then_inc(s["S"], 1)
                        elif kind == "PV":
                            _, g, h, j = step
                            n = j * HG + h
                            like = ("S", g, h, j, pieces(banded, j) - 1)
                            if n == 0:
                                if g:
                                    wait(pe, s["ote"], b, count("ote", ("ote", g - 1)))
                                else:
                                    wait(pe, s["ote"], b, count("ote", ("ote", G - 1), back=1))
                                    wait(pe, s["aux_dve"], b, count("aux_dve", ("v", NT // 2 - 1)))
                            if not banded:
                                wait(pe, masked, b, count("PV", step))
                            if banded or like[4]:
                                wait(pe, probs_ready, b, count("S", like))
                            lo, hi = j * P, j * P + width(j)
                            while lo < hi:
                                top = min(hi, (lo // 512 + 1) * 512)
                                first = j == (0 if (lo < 512 or not banded) else 1)
                                ins = pe.matmul(outT_ps[32 * h:32 * h + HD + 1, lo:top], v1[:, j, HG * g + h, :],
                                                probs[n % NP][:, lo - j * P:top - j * P], start=first, stop=j == NT - 1,
                                                skip_group_check=True)
                                lo = top
                            ins.then_inc(s["PV"], 1)
                        elif kind == "zt":
                            i2 = step[1]
                            wait(pe, s["z"], b, count("z", ("z", i2)))
                            for ii in range(2):
                                for kd in range(KD):
                                    ins = pe.transpose(dst[:, (ii * KD + kd) * P:(ii * KD + kd + 1) * P],
                                                       zb[:, i2 % 2, ii, kd * P:(kd + 1) * P], ident[:, :])
                            ins.then_inc(s["aux"], 1)
                        elif kind in ("q", "k"):
                            _, g, c = step
                            if g == G:
                                wait(pe, s["aux_dve"], b, count("aux_dve", ("zt", NT // 2 - 1)))
                            for kd in range(KD):
                                ins = pe.matmul(dst[:, :], wqk[:, 0 if kind == "q" else 1, kd, g * HG % H:g * HG % H + 8, :].rearrange("p h d -> p (h d)"),
                                                zT[:, kd, c * 512:(c + 1) * 512], start=kd == 0, stop=kd == KD - 1)
                            ins.then_inc(s["aux"], 1)
                        elif kind in ("v", "gate"):
                            i2 = step[1]
                            for ii in range(2):
                                tile = slice((2 * i2 + ii) * P, (2 * i2 + ii + 1) * P)
                                for kd in range(KD):
                                    rhs = wv[:, kd, :, :].rearrange("p h d -> p (h d)") if kind == "v" else wgate[:, kd, :]
                                    ins = pe.matmul(dst[:, ii * D:(ii + 1) * D], zT[:, kd, tile], rhs,
                                                    start=kd == 0, stop=kd == KD - 1)
                            ins.then_inc(s["aux"], 1)
                        elif kind == "mx":
                            _, g, h, i, c = step
                            if h == 0 and i == 0:
                                wait(pe, stacked, b, count("stack", ("stack", g), each=STACK))
                            if banded:
                                k0, wid = max(0, (i + 1) * P - SPAN), min(SPAN, (i + 1) * P)
                            else:
                                k0, wid = 512 * c, min(512, (i + 1) * P - 512 * c)
                            pe.matmul(dst[:, 0:wid], q_stack[g % 2][0:QK_ROWS, h, i * P:(i + 1) * P], k_stack[g % 2][0:QK_ROWS, h, k0:k0 + wid],
                                      start=True, stop=True).then_inc(s["aux"], 1)
                        elif kind == "mt":
                            wait(pe, s["mred"], b, count("mred", ("mred", step[1])))
                            pe.transpose(dst[:, :].bitcast(BF16)[0:PARTS * HG * NT, 0:P],
                                         neg_max_parts[:, :, :, :].rearrange("p a h i -> p (a h i)"), ident16[:, :]).then_inc(s["aux"], 1)
                        elif kind == "ot":
                            _, g, c = step
                            wait(pe, s["ote"], b, count("ote", ("ote", g), back=1 if g == G - 1 else 0))
                            for i in range(4):
                                ins = pe.transpose(dst[:, i * P:(i + 1) * P], outT[:, (4 * c + i) * P:(4 * c + i + 1) * P], ident[:, :])
                            ins.then_inc(s["aux"], 1)
                        elif kind == "at":
                            i2 = step[1]
                            if i2 == 0:
                                if banded:
                                    wait(pe, s["gmul"], b, count("gmul", ("gmul",)))
                                else:
                                    wait(pe, s["aux_dve"], b, count("aux_dve", ("ot", 3, 1)))
                            for ii in range(2):
                                for kd in range(KD):
                                    ins = pe.transpose(dst[:, (ii * KD + kd) * P:(ii * KD + kd + 1) * P],
                                                       flat[:, 2 * i2 + ii, kd * P:(kd + 1) * P], ident[:, :])
                            ins.then_inc(s["aux"], 1)
                        elif kind == "op":
                            i2 = step[1]
                            wait(pe, s["aux_act"], b, count("aux_act", ("at", i2)))
                            for ii in range(2):
                                for kd in range(KD):
                                    pe.matmul(dst[:, ii * D:(ii + 1) * D], flatT[:, i2 % 2, (ii * KD + kd) * P:(ii * KD + kd + 1) * P],
                                              wout[:, kd, :], start=kd == 0, stop=False)
                                ins = pe.matmul(dst[:, ii * D:(ii + 1) * D], ones_row[:, :], bout[:, :], start=False, stop=True)
                            ins.then_inc(s["aux"], 1)

                batches(pe, emit)



SLOTS = 4
QUADS = NE // 4


def ffn(nc, x_sb, ident, w, tag):
    with ExitStack() as ctx:
        sb = lambda name, shape, dt=F32: ctx.enter_context(nc.sbuf_tensor(tag + name, shape, dt))
        sem = lambda name: ctx.enter_context(nc.semaphore(tag + name))
        mv = sb("mv", [P, B * NT, 2])
        rstd = sb("rstd", [P, B * NT])
        gate_wT = sb("gate_wT", [P, KD, NE])
        gate_b = sb("gate_b", [P, 1])
        b1T = sb("b1T", [P, HE // P, NE])
        b2 = sb("b2", [P, D])
        wT = sb("wT", [P, 2, N])
        wtok = sb("wtok", [P, NT, 2, P])
        mergedT = sb("mergedT", [P, KD, NE, B])
        w1_ring = sb("w1_ring", [P, SLOTS, KD, HE])
        w2_ring = sb("w2_ring", [P, SLOTS, HE // P, D])
        w1_in = [sem(f"w1_in{n}") for n in range(SLOTS)]
        w2_in = [sem(f"w2_in{n}") for n in range(SLOTS)]
        o_experts = sb("o_experts", [P, QUADS, D])
        o_batch = sb("o_batch", [P, 2, D])
        bank = [ctx.enter_context(nc.psum_tensor(f"{tag}ps{n}", [P, 512], F32)) for n in range(8)]

        def load_expert(eng, e, n):
            eng.dma_start(w1_ring[:, n, :, :], w["w1"][bass.ds(e, 1), 0:D, :].rearrange("a (p k) h -> p (a k) h", k=KD)
                          ).then_inc(w1_in[n], 16)
            eng.dma_start(w2_ring[:, n, :, :], w["w2"][bass.ds(e, 1), 0:HE, :].rearrange("a (p c) d -> p (a c) d", c=HE // P)
                          ).then_inc(w2_in[n], 16)

        with ExitStack() as setup:
            ssb = lambda name, shape: setup.enter_context(nc.sbuf_tensor(tag + name, shape, F32))
            stats, std = ssb("stats", [P, B * NT, 6]), ssb("std", [P, B * NT])
            b1 = ssb("b1", [NE, HE])
            gw = ssb("gw", [NE, D])
            small_in, stat_steps, std_ready, turned, copied = (
                setup.enter_context(nc.semaphore(tag + n)) for n in ("small_in", "stat_steps", "std_ready", "turned", "copied"))
            with nc.Block() as block:
                @block.sync
                def _(sp):
                    sp.dma_start(b1[:, :], w["w1"][:, D, :]).then_inc(small_in, 16)
                    sp.dma_start(gw[:, :], w["gate_w"]).then_inc(small_in, 16)
                    for q in range(4):
                        sp.dma_start(b2[32 * q:32 * q + NE, :], w["w2"][:, HE, :]).then_inc(small_in, 16)
                        with nc.allow_non_contiguous_dma(reason="32 biases"):
                            sp.dma_start(gate_b[32 * q:32 * q + NE, :], w["gate_b"].rearrange("(e a) -> e a", a=1)).then_inc(small_in, 16)
                    for n in range(SLOTS):
                        load_expert(sp, n, n)

                @block.scalar
                def _(act):
                    act.wait_ge(stat_steps, STATS_STEPS)
                    act.activation(std[:, :], std[:, :], ACT.Sqrt).then_inc(std_ready, 1)

                @block.tensor
                def _(pe):
                    pe.wait_ge(small_in, 160)
                    for c in range(HE // P):
                        pe.transpose(bank[0][:, c * NE:(c + 1) * NE], b1[:, c:HE:HE // P], ident[0:NE, 0:NE])
                    for kd in range(KD):
                        ins = pe.transpose(bank[1][:, kd * NE:(kd + 1) * NE], gw[:, kd * P:(kd + 1) * P], ident[0:NE, 0:NE])
                    ins.then_inc(turned, 1)

                @block.vector
                def _(dve):
                    layer_norm_stats(dve, std_ready, stat_steps, x_sb, stats, mv, std, rstd)
                    dve.wait_ge(turned, 1)
                    dve.tensor_copy(b1T[:, :, :].rearrange("p c e -> p (c e)"), bank[0][:, 0:HE // P * NE]).then_inc(copied, 1)
                    dve.tensor_copy(gate_wT[:, :, :].rearrange("p k e -> p (k e)"), bank[1][:, 0:KD * NE]).then_inc(copied, 1)

        with ExitStack() as choose:
            ssb = lambda name, shape: choose.enter_context(nc.sbuf_tensor(tag + name, shape, F32))
            ssem = lambda name: choose.enter_context(nc.semaphore(tag + name))
            zb = ssb("zb", [P, 4, D])
            zT = ssb("zT", [P, 2, KD, 512])
            logits, marked = ssb("logits", [P, 2, N]), ssb("marked", [P, N])
            top, neg_max, total, inv = (ssb(n, [P, 2, m]) for n, m in (("top", TOPK), ("neg_max", 1), ("total", 1), ("inv", 1)))
            merged = ssb("merged", [P, 2, D])
            z_ready, z_turned, zT_ready, logits_done, logits_ready = (
                ssem(n) for n in ("z_ready", "z_turned", "zT_ready", "logits_done", "logits_ready"))
            top_steps, exp_ready, w_ready, w_turned, wtok_ready = (
                ssem(n) for n in ("top_steps", "exp_ready", "w_ready", "w_turned", "wtok_ready"))
            merge_done, merged_ready, merged_turned = (ssem(n) for n in ("merge_done", "merged_ready", "merged_turned"))
            CH = B * NT // 4
            with nc.Block() as block:
                @block.tensor
                def _(pe):
                    def logit(c):
                        b, half = c // 2, c % 2
                        pe.wait_ge(zT_ready, c + 1)
                        if c >= 2:
                            pe.wait_ge(logits_ready, c - 1)
                        for kd in range(KD):
                            ins = pe.matmul(bank[2 + c % 2][32 * (b % 4):32 * (b % 4) + NE, :], gate_wT[:, kd, :],
                                            zT[:, c % 2, kd, :], start=kd == 0, stop=kd == KD - 1)
                        ins.then_inc(logits_done, 1)

                    for c in range(CH):
                        for ii in range(4):
                            t = 4 * c + ii
                            pe.wait_ge(z_ready, t + 1)
                            if t >= 8 and ii % 2 == 0:
                                pe.wait_ge(zT_ready, (t - 8) // 4 + 1)
                            for kd in range(KD):
                                ins = pe.transpose(bank[(0, 1, 4, 5)[t // 2 % 4]][:, (ii % 2 * KD + kd) * P:(ii % 2 * KD + kd + 1) * P],
                                                   zb[:, t % 4, kd * P:(kd + 1) * P], ident[:, :])
                            ins.then_inc(z_turned, 1)
                        if c:
                            logit(c - 1)
                    logit(CH - 1)
                    for gq in range(2):
                        pe.wait_ge(w_ready, gq + 1)
                        for half in range(2):
                            for ii in range(4):
                                i = 4 * half + ii
                                ins = pe.transpose(bank[4 * gq + half][:, ii * P:(ii + 1) * P], wT[:, gq, i * P:(i + 1) * P], ident[:, :])
                            ins.then_inc(w_turned, 1)
                    for t in range(B * NT):
                        b, i = t // NT, t % NT
                        if t == 0:
                            pe.wait_ge(wtok_ready, 4)
                        pe.wait_ge(z_ready, B * NT + t + 1)
                        q = b % 4
                        pe.matmul(bank[2 + b // 4][32 * q:32 * q + NE, 0:D], wtok[:, i, b // 4, 32 * q:32 * q + NE],
                                  zb[:, t % 4, :], start=i == 0, stop=i == NT - 1).then_inc(merge_done, 1)
                    pe.wait_ge(merged_ready, 2)
                    for gq in range(2):
                        for kd in range(KD):
                            ins = pe.transpose(bank[0][:, (gq * KD + kd) * P:(gq * KD + kd + 1) * P], merged[:, gq, kd:D:KD], ident[:, :])
                    ins.then_inc(merged_turned, 1)

                @block.scalar
                def _(act):
                    for c in range(CH):
                        if c >= 2:
                            act.wait_ge(logits_done, c - 1)
                        for pair in range(2):
                            act.wait_ge(z_turned, 4 * c + 2 * pair + 2)
                            ins = act.activation(
                                zT[:, c % 2, :, 2 * pair * P:2 * (pair + 1) * P].rearrange("p k (i q) -> p i k q", q=P),
                                bank[(0, 1, 4, 5)[(2 * c + pair) % 4]][:, :].rearrange("p (i k q) -> p i k q", i=2, k=KD), ACT.Copy)
                        ins.then_inc(zT_ready, 1)
                    for gq in range(2):
                        act.wait_ge(top_steps, 1 + 3 * gq + 1)
                        act.activation(wT[:, gq, :], logits[:, gq, :], ACT.Exp, bias=neg_max[:, gq, :],
                                       accum_out=total[:, gq, :]).then_inc(exp_ready, 1)
                    for gq in range(2):
                        for half in range(2):
                            act.wait_ge(w_turned, 2 * gq + half + 1)
                            act.activation(wtok[:, 4 * half:4 * half + 4, gq, :],
                                           bank[4 * gq + half][:, :].rearrange("p (i q) -> p i q", q=P), ACT.Copy).then_inc(wtok_ready, 1)

                @block.vector
                def _(dve):
                    def z_tile(t):
                        dve.tensor_scalar(zb[:, t % 4, :], x_sb[:, t, :], mv[:, t, 0:1], rstd[:, t:t + 1],
                                          ALU.subtract, ALU.mult).then_inc(z_ready, 1)

                    def logits_of(c):
                        b, half = c // 2, c % 2
                        rows = slice(32 * (b % 4), 32 * (b % 4) + NE)
                        dve.wait_ge(logits_done, c + 1)
                        dve.tensor_scalar(logits[rows, b // 4, half * 512:(half + 1) * 512], bank[2 + c % 2][rows, :],
                                          gate_b[rows, :], None, ALU.add).then_inc(logits_ready, 1)

                    for c in range(CH):
                        for t in range(4 * c, 4 * c + 4):
                            if t >= 4:
                                dve.wait_ge(z_turned, t - 3)
                            z_tile(t)
                        if c >= 2:
                            logits_of(c - 2)
                    logits_of(CH - 2)
                    logits_of(CH - 1)
                    dve.wait_ge(logits_ready, CH)
                    for gq in range(2):
                        dve.max(top[:, gq, :], logits[:, gq, :]).then_inc(top_steps, 1)
                        dve.wait_ge(top_steps, 3 * gq + 1)
                        dve.tensor_scalar(neg_max[:, gq, :], top[:, gq, 0:1], -1.0, None, ALU.mult).then_inc(top_steps, 1)
                        if gq:
                            dve.wait_ge(w_ready, gq)
                        dve.match_replace(marked[:, :], top[:, gq, :], logits[:, gq, :], LOWEST).then_inc(top_steps, 1)
                        dve.wait_ge(exp_ready, gq + 1)
                        dve.wait_ge(top_steps, 3 * gq + 3)
                        dve.reciprocal(inv[:, gq, :], total[:, gq, :]).then_inc(logits_ready, 1)
                        dve.scalar_tensor_tensor(out=wT[:, gq, :], in0=marked[:, :], scalar=LOWEST, in1=wT[:, gq, :],
                                                 op0=ALU.is_equal, op1=ALU.mult).then_inc(logits_ready, 1)
                        dve.wait_ge(logits_ready, CH + 2 * gq + 2)
                        dve.tensor_scalar(wT[:, gq, :], wT[:, gq, :], inv[:, gq, :], None, ALU.mult).then_inc(w_ready, 1)
                    for t in range(B * NT):
                        if t >= 4:
                            dve.wait_ge(merge_done, t - 3)
                        z_tile(t)
                    dve.wait_ge(merge_done, B * NT)
                    for gq in range(2):
                        dve.tensor_copy(merged[:, gq, :], bank[2 + gq][:, 0:D]).then_inc(merged_ready, 1)
                    dve.wait_ge(merged_turned, 1)
                    for gq in range(2):
                        for kd in range(KD):
                            c0 = (gq * KD + kd) * P
                            dve.tensor_copy(mergedT[:, kd, :, 4 * gq:4 * gq + 4],
                                            bank[0][:, c0:c0 + P].rearrange("p (b e) -> p e b", e=NE)).then_inc(logits_ready, 1)

        with ExitStack() as run:
            rsb = lambda name, shape: run.enter_context(nc.sbuf_tensor(tag + name, shape, F32))
            rsem = lambda name: run.enter_context(nc.semaphore(tag + name))
            lhs1 = [rsb(f"lhs1_{n}", [P, KD, 4, 32]) for n in range(2)]
            hid = [rsb(f"hid{n}", [P, HE]) for n in range(2)]
            hidT = [rsb(f"hidT{n}", [P, HE // P, 4, 32]) for n in range(2)]
            pre = rsb("pre", [P, HE // P, 4, B])
            cleared, lhs1_ready, hid_done, hid_ready, hid_turned, pre_ready, hidT_ready, out_done, out_ready, moved = (
                rsem(n) for n in ("cleared", "lhs1_ready", "hid_done", "hid_ready", "hid_turned", "pre_ready",
                                  "hidT_ready", "out_done", "out_ready", "moved"))
            scattered, summed, o_ready = (rsem(n) for n in ("scattered", "summed", "o_ready"))

            with nc.Block() as block:
                def pairs(eng, emit):
                    emit(0)
                    with eng.Fori(1, QUADS // 2) as it:
                        emit(it)

                @block.sync
                def _(sp):
                    with sp.Fori(0, QUADS - 1) as q:
                        for j in range(4):
                            sp.wait_ge(out_done, q * 4 + j + 1)
                            load_expert(sp, q * 4 + j + SLOTS, j)
                    sp.wait_ge(out_ready, QUADS)
                    for b in range(B):
                        for j in range(4):
                            r0 = 32 * (b % 4) + j
                            sp.dma_start(o_batch[r0:r0 + NE - 3:4, b // 4, :], o_experts[32 * j + b:32 * j + b + 1, :, :]).then_inc(moved, 16)
                    sp.wait_ge(moved, 16 * 4 * B)

                @block.gpsimd
                def _(pool):
                    for n in range(2):
                        pool.memset(lhs1[n][:, :, :, :], 0.0).then_inc(cleared, 1)
                        pool.memset(hidT[n][:, :, :, :], 0.0).then_inc(cleared, 1)
                    pool.wait_ge(cleared, 4)

                    def emit(it):
                        for half in range(2):
                            wait(pool, hid_done, it, lambda i: 2 * i + half - 1 if 2 * i + half >= 2 else None)
                            pool.tensor_copy(lhs1[half][:, :, :, 0:B],
                                             mergedT[:, :, bass.ds(it * 8 + 4 * half, 4), :]).then_inc(lhs1_ready, 1)
                    pairs(pool, emit)

                @block.tensor
                def _(pe):
                    pe.wait_ge(cleared, 4)

                    def up(it, half):
                        wait(pe, lhs1_ready, it, lambda i: 2 * i + half + 1)
                        wait(pe, hid_ready, it, lambda i: 2 * i + half if 2 * i + half else None)
                        for j in range(4):
                            wait(pe, w1_in[j], it, lambda i: 16 * (2 * i + half + 1))
                            for n in range(2):
                                for kd in range(KD):
                                    ins = pe.matmul(bank[n][32 * j:32 * j + 32, :], lhs1[half][:, kd, j, :],
                                                    w1_ring[:, j, kd, n * 512:(n + 1) * 512], start=kd == 0, stop=kd == KD - 1)
                        ins.then_inc(hid_done, 1)

                    def turn(it, half):
                        wait(pe, hid_ready, it, lambda i: 2 * i + half + 1)
                        wait(pe, pre_ready, it, lambda i: 2 * i + half if 2 * i + half else None)
                        for c in range(HE // P):
                            ins = pe.transpose(bank[2 + c // 4][:, c % 4 * P:(c % 4 + 1) * P], hid[half][:, c:HE:HE // P], ident[:, :])
                        ins.then_inc(hid_turned, 1)

                    def down(it, half):
                        wait(pe, hidT_ready, it, lambda i: 2 * i + half + 1)
                        if half == 0:
                            wait(pe, out_ready, it, lambda i: 2 * i - 1 if i else None)
                        else:
                            wait(pe, out_ready, it, lambda i: 2 * i if i else None)
                        for j in range(4):
                            wait(pe, w2_in[j], it, lambda i: 16 * (2 * i + half + 1))
                            for c in range(HE // P):
                                ins = pe.matmul(bank[4 + half][32 * j:32 * j + 32, 0:D], hidT[half][:, c, j, :],
                                                w2_ring[:, j, c, :], start=c == 0, stop=c == HE // P - 1)
                            ins.then_inc(out_done, 1)

                    def emit(it):
                        for half in range(2):
                            up(it, half)
                            turn(it, half)
                            down(it, half)
                    pairs(pe, emit)

                    pe.wait_ge(o_ready, 1)
                    for t2 in range(B * NT // 2):
                        if t2 >= 2:
                            pe.wait_ge(summed, t2 - 1)
                        for ii in range(2):
                            b, i = (2 * t2 + ii) // NT, (2 * t2 + ii) % NT
                            rows = slice(32 * (b % 4), 32 * (b % 4) + NE)
                            ins = pe.matmul(bank[6 + t2 % 2][:, ii * D:(ii + 1) * D], wT[rows, b // 4, i * P:(i + 1) * P],
                                            o_batch[rows, b // 4, :], start=True, stop=True)
                        ins.then_inc(scattered, 1)

                @block.scalar
                def _(act):
                    def emit(it):
                        for half in range(2):
                            wait(act, hid_done, it, lambda i: 2 * i + half + 1)
                            wait(act, hid_turned, it, lambda i: 2 * i + half - 1 if 2 * i + half >= 2 else None)
                            for n in range(2):
                                ins = act.activation(hid[half][:, n * 512:(n + 1) * 512], bank[n][:, :], ACT.Copy)
                            ins.then_inc(hid_ready, 1)
                            wait(act, pre_ready, it, lambda i: 2 * i + half + 1)
                            wait(act, out_done, it, lambda i: 4 * (2 * i + half - 1) if 2 * i + half >= 2 else None)
                            act.activation(hidT[half][:, :, :, 0:B], pre[:, :, :, :], ACT.Gelu).then_inc(hidT_ready, 1)
                            wait(act, out_done, it, lambda i: 4 * (2 * i + half + 1))
                            act.activation(o_experts[:, bass.ds(2 * it + half, 1), :].rearrange("p a d -> p (a d)"),
                                           bank[4 + half][:, 0:D], ACT.Copy).then_inc(out_ready, 1)
                    pairs(act, emit)

                @block.vector
                def _(dve):
                    def emit(it):
                        for half in range(2):
                            wait(dve, hid_turned, it, lambda i: 2 * i + half + 1)
                            wait(dve, hidT_ready, it, lambda i: 2 * i + half if 2 * i + half else None)
                            for n in range(2):
                                ins = dve.tensor_tensor(
                                    pre[:, 4 * n:4 * n + 4, :, :],
                                    bank[2 + n][:, :].rearrange("p (c j r) -> p c j r", c=4, j=4)[:, :, :, 0:B],
                                    b1T[:, 4 * n:4 * n + 4, bass.ds(it * 8 + 4 * half, 4)].unsqueeze(3).to_broadcast([P, 4, 4, B]), ALU.add)
                            ins.then_inc(pre_ready, 1)
                    pairs(dve, emit)
                    dve.wait_ge(moved, 16 * 4 * B)
                    for gq in range(2):
                        ins = dve.tensor_tensor(o_batch[:, gq, :], o_batch[:, gq, :], b2[:, :], ALU.add)
                    ins.then_inc(o_ready, 1)
                    for t2 in range(B * NT // 2):
                        dve.wait_ge(scattered, t2 + 1)
                        xt = x_sb[:, 2 * t2:2 * t2 + 2, :].rearrange("p i d -> p (i d)")
                        dve.tensor_tensor(xt, bank[6 + t2 % 2][:, :], xt, ALU.add).then_inc(summed, 1)


def store(nc, x_sb, out):
    with nc.semaphore("stored") as stored, nc.Block() as block:
        @block.sync
        def _(sp):
            for b in range(B):
                sp.dma_start(out[b].rearrange("(i p) d -> p i d", p=P), x_sb[:, b * NT:(b + 1) * NT, :]).then_inc(stored, 16)
            sp.wait_ge(stored, 16 * B)


STAGES = ("a", "f", "b", "f2")


def build(nc, a, out):
    scratch = {n: nc.dram_tensor(n + "_dram", [H, P, LINE], dt) for n, dt in (("line_k", F32), ("line_q", BF16))}
    scratch["parts"] = nc.dram_tensor("parts_dram", [2, 2, PARTS, P, N], BF16)
    attn_a = {"qkv": a["L0_attn_a_Wqkv"], "bqkv": a["L0_attn_a_bqkv"], "out": a["L0_attn_a_Wout"], "bout": a["L0_attn_a_bout"],
              "gate": a["L0_attn_a_Wgate"], "bgate": a["L0_attn_a_bgate"], "pos_bias": a["L0_attn_a_pos_bias"]}
    attn_b = {"qkv": a["L0_attn_b_W1"], "bqkv": a["L0_attn_b_b1"], "out": a["L0_attn_b_W2"], "bout": a["L0_attn_b_b2"]}
    experts = {"gate_w": a["L0_ffn_gate_w"], "gate_b": a["L0_ffn_gate_b"], "w1": a["L0_ffn_w1"], "w2": a["L0_ffn_w2"]}
    with nc.sbuf_tensor("x_sb", [P, B * NT, D], F32) as x_sb, nc.sbuf_tensor("ident", [P, P], F32) as ident:
        build_constants(nc, ident, a["L0_attn_a_x"], x_sb)
        if "a" in STAGES:
            attention(nc, x_sb, ident, attn_a, True, scratch)
        if "f" in STAGES:
            ffn(nc, x_sb, ident, experts, "f1_")
        if "b" in STAGES:
            attention(nc, x_sb, ident, attn_b, False, scratch)
        if "f2" in STAGES:
            ffn(nc, x_sb, ident, experts, "f2_")
        store(nc, x_sb, out)


_INS = ["L0_attn_a_x", "L0_attn_a_Wqkv", "L0_attn_a_bqkv", "L0_attn_a_Wout", "L0_attn_a_bout", "L0_attn_a_Wgate",
        "L0_attn_a_bgate", "L0_attn_a_pos_bias", "L0_attn_b_W1", "L0_attn_b_b1", "L0_attn_b_W2", "L0_attn_b_b2",
        "L0_ffn_gate_w", "L0_ffn_gate_b", "L0_ffn_w1", "L0_ffn_w2"]


def kernel(**inputs):
    import numpy as _np
    import concourse.bacc as _bacc
    from concourse import mybir as _mybir
    from concourse.bass_utils import run_bass_kernel_spmd as _run

    nc = _bacc.Bacc("TRN2", target_bir_lowering=False, num_devices=1, dynamic_dma_scratch_size=256)
    arrays, args = {}, {}
    for name in _INS:
        a = _np.ascontiguousarray(inputs[name])
        arrays[f"in_{name}_dram"] = a
        args[name] = nc.dram_tensor(f"in_{name}_dram", a.shape, _mybir.dt.from_np(a.dtype), kind="ExternalInput").ap()
    out = nc.dram_tensor("out_0_dram", (8, 1024, 256), _mybir.dt.float32, kind="ExternalOutput").ap()
    build(nc, args, out)
    r = _run(nc, [arrays], core_ids=[0])
    return r.results[0]["out_0_dram"]
```

```python
from contextlib import ExitStack

import concourse.bass as bass
from concourse import mybir

P = 128
F32 = mybir.dt.float32
BF16 = mybir.dt.bfloat16
ALU = mybir.AluOpType
ACT = mybir.ActivationFunctionType
AX = mybir.AxisListType

B, N, D = 8, 1024, 256
NT = N // P
KD = D // P
H, HD = 16, 16
G, HG = 4, 4
PARTS = 3
PART_PAIRS = ((0, 0), (1, 1), (2, 0), (0, 1), (1, 0), (0, 2))
QK_ROWS = len(PART_PAIRS) * HD
ALL_ROWS = QK_ROWS + PARTS
NE, HE, TOPK = 32, 1024, 8
EPS = 1e-5
NEG = -1e30
LOWEST = -3e38
OFFSETS = sorted(set(range(33)) | {48, 64, 96, 128, 192, 256, 384})
SPAN = 512
LINE = SPAN + P


def windows(ap, h, heads):
    return bass.AP(ap.tensor, h * P * LINE + P - 1, [[LINE - 1, P], [P * LINE, heads], [1, SPAN]])


def runs(which):
    out = []
    for r, pair in enumerate(PART_PAIRS):
        if out and pair[which] == out[-1][1] + out[-1][2]:
            out[-1][2] += 1
        else:
            out.append([r, pair[which], 1])
    return out


def at_iteration(b, count):
    if isinstance(b, int):
        return count(b)
    first, second = count(1), count(2)
    return b * (second - first) + (first - (second - first))


def wait_alone(eng, sem, b, count, passed):
    wait(eng, sem, b, count)
    if not isinstance(b, int):
        eng.sem_inc(passed, 1)


def wait(eng, sem, b, count):
    value = at_iteration(b, count)
    if isinstance(b, int) and not value:
        return
    eng.wait_ge(sem, value)



def build_constants(nc, ident, x, x_sb, stats):
    with ExitStack() as ctx:
        x_loaded = [ctx.enter_context(nc.semaphore(f"x_loaded{b}")) for b in range(B)]
        ident_steps = ctx.enter_context(nc.semaphore("ident_steps"))
        block = ctx.enter_context(nc.Block())

        @block.sync
        def _(sp):
            for b in range(B):
                sp.dma_start(x_sb[:, b * NT:(b + 1) * NT, :],
                             x[b].rearrange("(i p) d -> p i d", p=P)).then_inc(x_loaded[b], 16)

        @block.vector
        def _(dve):
            for b in range(B):
                dve.wait_ge(x_loaded[b], 16)
                for t in range(b * NT, (b + 1) * NT):
                    dve.bn_stats(stats[:, t, :], x_sb[:, t, :])

        @block.gpsimd
        def _(pool):
            pool.memset(ident[:, :], 0.0).then_inc(ident_steps, 1)
            pool.wait_ge(ident_steps, 1)
            pool.affine_select(out=ident[:, :], in_=ident[:, :], compare_op=ALU.not_equal, fill=1.0, base=0,
                               pattern=[[-1, P]], channel_multiplier=1).then_inc(ident_steps, 1)
            pool.wait_ge(ident_steps, 2)


def layer_norm_stats(dve, act_sem, dve_sem, stats, mv, std, rstd):
    done = 0
    for t in range(B * NT):
        dve.bn_aggr(mv[:, t, :], stats[:, t, :]).then_inc(dve_sem, 1)
    done += B * NT
    dve.wait_ge(dve_sem, done)
    dve.tensor_scalar(std[:, :], mv[:, :, 1], EPS, None, ALU.add).then_inc(dve_sem, 1)
    done += 1
    dve.wait_ge(act_sem, 1)
    dve.reciprocal(rstd[:, :], std[:, :]).then_inc(dve_sem, 1)
    return done


STATS_STEPS = B * NT + 1



def pieces(banded, j):
    return 1 if banded or N - j * P <= 512 else 2


def key_order(banded):
    return tuple(range(NT)) if banded else (0, 7, 1, 6, 2, 5, 3, 4)


def attention_schedule(banded):
    def projections(g):
        out = []
        for kind in "qk":
            out += [(step, g, c) if step == kind else (step, g, kind, c)
                    for step in (kind, "rest1", "part1", "part2") for c in range(2)]
            out.append(("spill", g, kind))
        return out

    def operands(g):
        return ([("bias", g)] if banded else []) + [("stack", g)]

    def row_maxima(g):
        return [("mx", g, h, i, c) for h in range(HG) for i in range(NT)
                for c in range(1 if banded or i < 4 else 2)] + [("mred", g)] + MRED_STEPS[banded] * [None] + [("mt", g), ("mrow", g)]

    def tokens():
        out = []
        for i2 in range(NT // 2):
            out += [("z", i2), ("zt", i2)]
        return out

    def outputs(beside=()):
        out = [("ot", 3, 0), ("ot", 3, 1)] + ([("gmul",)] if banded else []) + list(beside)
        return out + [("at", 0), ("at", 1), ("op", 0), ("at", 2), ("op", 1), ("at", 3), ("op", 2), ("op", 3)]

    def statistics():
        return [("stats", i2) for i2 in range(NT // 2)]

    def body(b):
        out = []
        pending = []
        slots = HG * NT
        order = key_order(banded)
        cost = [min(SPAN if banded else N, N - order[s // HG] * P) + P for s in range(slots)]
        for g in range(G):
            others = [] if g == 0 else [("ot", g - 1, 0), ("ot", g - 1, 1)]
            if g == 0:
                others += outputs(projections(2)) if b else projections(2) + PROJECTIONS_AHEAD * [None]
            if g == 1 and banded:
                others += [("gate", i2) for i2 in range(NT // 2)]
            if g == 1 and b:
                others += statistics()
            if g == TOKENS_IN and b < B - 1:
                others += tokens()
            if g == 2 and b < B - 1:
                others += projections(4) + PROJECTIONS_AHEAD * [None]
            maxima = row_maxima(g + 1) if g < G - 1 or b < B - 1 else []
            if maxima:
                out += operands(g + 1)
            streams = [[maxima, 0, MAXIMA_FROM[banded], MAXIMA_TO[banded]], [others, 0, 0.1, OTHERS_TO]]
            for s in range(slots):
                h, j = s % HG, order[s // HG]
                out += [("S", g, h, j, c) for c in range(pieces(banded, j))]
                pending.append(("PV", g, h, j))
                if g == 0 and s == 2:
                    out += [("v", i2) for i2 in range(NT // 2)]
                if s % PV_RUN == PV_RUN - 1 and len(pending) > PV_LAG:
                    out += pending[:PV_RUN]
                    del pending[:PV_RUN]
                    if out[-1][2:] == (HG - 1, order[-1]):
                        out.append(("ote", out[-1][1]))
                share = sum(cost[:s + 1]) / sum(cost)
                for stream in streams:
                    work, taken, start, stop = stream
                    upto = min(len(work), max(taken, int(len(work) * (share - start) / (stop - start)))) if s > HG else 0
                    if s == slots - 1:
                        upto = len(work)
                    out += [step for step in work[taken:upto] if step]
                    stream[1] = upto
        out += pending
        out.append(("ote", G - 1))
        return out

    seq = {-1: [step for step in tokens() + projections(4) + operands(4) + row_maxima(4) if step], B: outputs() + statistics()}
    for b in range(B):
        seq[b] = body(b)
    return seq


PV_RUN, PV_LAG = 4, 4
PROJECTIONS_AHEAD = 6
MRED_STEPS = {True: 1, False: 3}
TOKENS_IN = 1
MAXIMA_FROM, MAXIMA_TO = {True: 0.1, False: 0.05}, {True: 0.9, False: 0.94}
OTHERS_TO = 1.0



def attention(nc, x_sb, stats, ident, w, banded, scratch):
    seq = attention_schedule(banded)
    order = key_order(banded)
    AUX_DVE = ("mx", "mt", "ot", "op") + (() if banded else ("zt", "v"))
    AUX_ACT = ("q", "k", "at") + (("zt", "v", "gate") if banded else ())
    taker = lambda kind: "aux_dve" if kind in AUX_DVE else "aux_act"
    classes = {
        "aux": AUX_DVE + AUX_ACT, "aux_dve": AUX_DVE, "aux_act": AUX_ACT, "S": ("S",), "PV": ("PV",),
        **{kind: (kind,) for kind in ("ote", "z", "mred", "gmul", "ot", "rest1", "part1", "part2", "spill", "stack", "mrow", "bias")},
    }
    done = {c: {} for c in classes}
    slot_user = []
    for c, kinds in classes.items():
        n = 0
        for b in sorted(seq):
            for step in seq[b]:
                if step[0] in kinds:
                    n += 1
                    done[c][b, step] = n
    for b in sorted(seq):
        for step in seq[b]:
            if step[0] in classes["aux"]:
                slot_user.append(taker(step[0]))

    def count(c, step, back=0, minus=0, each=1, plus=0):
        def of(b):
            n = done[c].get((b - back, step))
            return None if n is None or n - minus <= 0 else each * (n - minus) + plus
        return of

    def slot_free(step):
        def of(b):
            n = done["aux"][b, step] - 1 - NA
            return None if n < 0 else slot_user[:n + 1].count(slot_user[n])
        def who(b):
            n = done["aux"][b, step] - 1 - NA
            return None if n < 0 else slot_user[n]
        return who, of

    def bank(b, step):
        b = 1 if not isinstance(b, int) else b
        return (done["aux"][b, step] - 1) % NA

    NA, NS = (4, 2) if banded else (3, 3)
    NP = 2 * HG
    PW = SPAN if banded else N
    col = {}
    if banded:
        wq_cols = lambda m, kd: w["qkv"][kd * P:(kd + 1) * P, m * D:(m + 1) * D].rearrange("p (h d) -> p h d", d=HD)
        bias_of = lambda m: w["bqkv"][m * D:(m + 1) * D].rearrange("(h d) -> h d", d=HD)
    else:
        wq_cols = lambda m, kd: w["qkv"][kd * P:(kd + 1) * P, :].rearrange("p (h m d) -> p h m d", m=3, d=HD)[:, :, m, :]
        bias_of = lambda m: w["bqkv"].rearrange("(h m d) -> h m d", m=3, d=HD)[:, m, :]

    with ExitStack() as ctx:
        tag = "a_" if banded else "b_"
        sb = lambda name, shape, dt=F32: ctx.enter_context(nc.sbuf_tensor(tag + name, shape, dt))
        sem = lambda name: ctx.enter_context(nc.semaphore(tag + name))

        wqk = sb("wqk", [P, 2, KD, H, HD])
        wv = sb("wv", [P, KD, H, HD])
        wout = sb("wout", [P, KD, D])
        bqk = sb("bqk", [P, 2, 2])
        ident16 = sb("ident16", [P, P], BF16)
        bv = sb("bv", [1 if banded else P, D])
        bout = sb("bout", [1, D])
        ones_row = sb("ones_row", [1, P])
        mv = sb("mv", [P, B * NT, 2])
        rstd = sb("rstd", [P, B * NT])
        if banded:
            wgate = sb("wgate", [P, KD, D])
            bgate = sb("bgate", [1, D])
            bias_k = [sb(f"bias_k{n}", [P, HG, SPAN]) for n in range(2)]
            bias_q = sb("bias_q", [P, H, SPAN], BF16)
            gate = sb("gate", [P, NT, D])
        else:
            causal = sb("causal", [P, SPAN])

        with ExitStack() as setup:
            ssb = lambda name, shape, dt=F32: setup.enter_context(nc.sbuf_tensor(tag + name, shape, dt))
            ssem = lambda name: setup.enter_context(nc.semaphore(tag + name))
            std = ssb("std", [P, B * NT])
            weights_in, stat_steps, std_ready = (ssem(n) for n in ("weights_in", "stat_steps", "std_ready"))
            pool_steps, small_steps, lines_out, bias_in, pos_in = (ssem(n) for n in ("pool_steps", "small_steps", "lines_out", "bias_in", "pos_in"))
            if banded:
                pos = ssb("pos", [H, len(OFFSETS)])
                line_k = ssb("line_k", [H, LINE])
                line_q = ssb("line_q", [H, LINE], BF16)
            n_loads = 2 * KD + (KD if not banded else 1) + 1 + 2 * 2 + 1 + 1 + (2 if banded else 0)
            with nc.Block() as block:
                @block.sync
                def _(sp):
                    with nc.allow_non_contiguous_dma(reason="heads' weights and biases, loaded once"):
                        for m in range(2):
                            for kd in range(KD):
                                sp.dma_start(wqk[:, m, kd, :, :], wq_cols(m, kd)).then_inc(weights_in, 16)
                            for half in range(2):
                                sp.dma_start(bqk[:, m, half:half + 1], bias_of(m)[8 * half:8 * half + 8, :]).then_inc(weights_in, 16)
                        if banded:
                            sp.dma_start(wv[:, :, :, :].rearrange("p k h d -> p k (h d)"),
                                         w["qkv"][:, 2 * D:3 * D].rearrange("(k p) n -> p k n", p=P)).then_inc(weights_in, 16)
                        else:
                            for kd in range(KD):
                                sp.dma_start(wv[:, kd, :, :], wq_cols(2, kd)).then_inc(weights_in, 16)
                        sp.dma_start(bv[:, :].rearrange("p (h d) -> p h d", d=HD),
                                     bass.AP(bias_of(2).tensor, bias_of(2).offset, [[0, bv.shape[0]]] + [list(a) for a in bias_of(2).ap])
                                     ).then_inc(weights_in, 16)
                    sp.dma_start(wout[:, :, :], w["out"].rearrange("(k p) n -> p k n", p=P)).then_inc(weights_in, 16)
                    sp.dma_start(bout[:, :], w["bout"].rearrange("(a n) -> a n", a=1)).then_inc(weights_in, 16)
                    if banded:
                        sp.dma_start(wgate[:, :, :], w["gate"].rearrange("(k p) n -> p k n", p=P)).then_inc(weights_in, 16)
                        sp.dma_start(bgate[:, :], w["bgate"].rearrange("(a n) -> a n", a=1)).then_inc(weights_in, 16)
                    sp.wait_ge(weights_in, 16 * n_loads)

                @block.gpsimd
                def _(pool):
                    pool.memset(ones_row[:, :], 1.0).then_inc(pool_steps, 1)
                    pool.memset(ident16[:, :], 0.0).then_inc(pool_steps, 1)
                    pool.wait_ge(pool_steps, 2)
                    pool.affine_select(out=ident16[:, :], in_=ident16[:, :], compare_op=ALU.not_equal, fill=1.0, base=0,
                                       pattern=[[-1, P]], channel_multiplier=1).then_inc(pool_steps, 1)
                    if not banded:
                        pool.memset(causal[:, :], 0.0).then_inc(pool_steps, 1)
                        pool.wait_ge(pool_steps, 4)
                        last = causal[:, SPAN - P:SPAN]
                        pool.affine_select(out=last, in_=last, compare_op=ALU.is_ge, fill=NEG, base=0,
                                           pattern=[[-1, P]], channel_multiplier=1).then_inc(pool_steps, 1)

                @block.scalar
                def _(act):
                    if banded:
                        with nc.allow_non_contiguous_dma(reason="640 biases, transposed"):
                            act.dma_start(pos[:, :], w["pos_bias"].rearrange("o h -> h o")).then_inc(pos_in, 16)
                        act.wait_ge(small_steps, 2 + 2 * len(OFFSETS))
                        act.dma_start(scratch["line_k"].ap(), line_k[:, :].unsqueeze(1).to_broadcast([H, P, LINE])).then_inc(lines_out, 16)
                        act.dma_start(scratch["line_q"].ap(), line_q[:, :].unsqueeze(1).to_broadcast([H, P, LINE])).then_inc(lines_out, 16)
                        act.wait_ge(lines_out, 32)
                        act.dma_start(bias_q[:, :, :], windows(scratch["line_q"].ap(), 0, H)).then_inc(bias_in, 16)
                    act.wait_ge(stat_steps, STATS_STEPS)
                    act.activation(std[:, :], std[:, :], ACT.Sqrt).then_inc(std_ready, 1)
                    if banded:
                        act.wait_ge(bias_in, 16)

                @block.vector
                def _(dve):
                    if banded:
                        dve.memset(line_k[:, :], NEG).then_inc(small_steps, 1)
                        dve.memset(line_q[:, :], NEG).then_inc(small_steps, 1)
                        dve.wait_ge(small_steps, 2)
                        dve.wait_ge(pos_in, 16)
                        for n, off in enumerate(OFFSETS):
                            k, q = off + P - 1, SPAN - 1 - off
                            dve.tensor_copy(line_k[:, k:k + 1], pos[:, n:n + 1]).then_inc(small_steps, 1)
                            dve.tensor_copy(line_q[:, q:q + 1], pos[:, n:n + 1]).then_inc(small_steps, 1)
                    layer_norm_stats(dve, std_ready, stat_steps, stats, mv, std, rstd)
                    dve.wait_ge(weights_in, 16 * n_loads)
                    dve.tensor_scalar(bqk[:, 0, :], bqk[:, 0, :], HD ** -0.5, None, ALU.mult).then_inc(stat_steps, 1)
                    if banded:
                        dve.tensor_scalar(bout[:, :], bout[:, :], 2.0, None, ALU.mult).then_inc(stat_steps, 1)

        zb = sb("zb", [P, 2, 2, D])
        zT = sb("zT", [P, KD, N])
        full = sb("full", [P, N])
        parts = [sb(f"parts{n}", [P, PARTS, N], BF16) for n in range(2)]
        q_stack = [sb(f"q_stack{n}", [ALL_ROWS, HG, N], BF16) for n in range(2)]
        k_stack = [sb(f"k_stack{n}", [ALL_ROWS, HG, N], BF16) for n in range(2)]
        v1 = sb("v1", [P, NT, H, HD + 1])
        probs = [sb(f"probs{n}", [P, PW]) for n in range(NP)]
        maxima = sb("maxima", [P, HG, NT, 2])
        neg_max = sb("neg_max", [P, HG, NT])
        neg_max_parts = sb("neg_max_parts", [P, PARTS, HG, NT], BF16)
        neg_max_rows = sb("neg_max_rows", [PARTS * HG * NT, P], BF16)
        outT = sb("outT", [P, N])
        recip = sb("recip", [P, 2, 4, HG])
        flat = sb("flat", [P, NT, D])
        flatT = sb("flatT", [P, 2, 4 * P])

        scoresT_ps = [ctx.enter_context(nc.psum_tensor(f"{tag}scoresT{n}", [P, 512], F32)) for n in range(NS)]
        outT_ps = ctx.enter_context(nc.psum_tensor(f"{tag}outT_ps", [P, N], F32))
        aux_ps = [ctx.enter_context(nc.psum_tensor(f"{tag}aux{n}", [P, 512], F32)) for n in range(NA)]

        cleared = sem("cleared")
        s = {c: sem(c) for c in ("aux", "aux_dve", "aux_act", "S", "PV", "ote", "z", "mred", "gmul", "rest1", "part1", "part2")}
        spilled, stacked, mrows_in, bias_in = (sem(n) for n in ("spilled", "stacked", "mrows_in", "bias_in"))
        SPILL, STACK, MROW, BIAS = 16 * PARTS, 16 * sum(len(runs(which)) for which in range(2)), 16, 16
        mred_chain = sem("mred_chain")
        added = sem("added")
        probs_ready = sem("probs_ready")
        masked = sem("masked")
        passed = sem("passed")
        dve_chain = sem("dve_chain")

        scores = [step for step in seq[1] if step[0] == "S"]

        def width(j):
            return min(PW, N - j * P)

        def piece(b, step):
            _, g, h, j, c = step
            return scoresT_ps[scores.index(step) % NS], 512 * c, min(512, width(j) - 512 * c)

        def tile_before(step):
            n = scores.index(step)
            return NS if n >= NS else n + len(scores) - max(m for m in range(len(scores)) if m % NS == n)

        def batches(eng, emit):
            emit(-1)
            emit(0)
            with eng.Fori(1, B - 1) as b:
                emit(b)
            emit(B - 1)
            emit(B)

        def steps(b):
            return seq[b if isinstance(b, int) else 1]

        def nth(b, c, step, minus=0):
            return count(c, step, 0, minus)

        with nc.Block() as block:
            @block.vector
            def _(dve):
                for n in range(2):
                    dve.memset(k_stack[n][QK_ROWS:ALL_ROWS, :, :], 1.0).then_inc(cleared, 1)
                dve.memset(maxima[:, :, :, :], LOWEST).then_inc(cleared, 1)
                dve.memset(v1[:, :, :, :], 1.0).then_inc(cleared, 1)
                dve.memset(outT_ps[:, :], 0.0).then_inc(cleared, 1)
                dve.wait_ge(cleared, 5)

                def emit(b):
                    for step in steps(b):
                        kind = step[0]
                        if kind == "S" and banded:
                            _, g, h, j, _ = step
                            n = order.index(j) * HG + h
                            if n == 0:
                                wait(dve, bias_in, b, count("bias", ("bias", g or G), back=0 if g else 1, each=BIAS))
                            wait(dve, s["S"], b, count("S", step))
                            wait(dve, s["PV"], b, count("PV", ("PV", g, h, j), minus=NP))
                            dve.tensor_tensor(probs[n % NP][:, 0:width(j)], piece(b, step)[0][:, 0:width(j)],
                                              bias_k[g % 2][:, h, 0:width(j)], ALU.add).then_inc(added, 1)
                        if kind == "z":
                            i2 = step[1]
                            if i2 >= 2:
                                wait(dve, s["aux"], b, count("aux", ("zt", i2 - 2)))
                            for ii in range(2):
                                tile = (b + 1) * NT + 2 * i2 + ii
                                ins = dve.tensor_scalar(zb[:, i2 % 2, ii, :], x_sb[:, bass.ds(tile, 1), :].rearrange("p a d -> p (a d)"),
                                                        mv[:, bass.ds(tile, 1), 0], rstd[:, bass.ds(tile, 1)],
                                                        ALU.subtract, ALU.mult)
                            ins.then_inc(s["z"], 1)
                        if kind == "mred":
                            g = step[1]
                            last = ("mx", g, HG - 1, NT - 1, 0 if banded else 1)
                            wait(dve, s["aux_dve"], b, count("aux_dve", last))
                            wait(dve, s["aux"], b, count("aux", ("mt", G if g == 1 else g - 1), back=1 if g == 1 else 0))

                            def chained(ins, n):
                                ins.then_inc(mred_chain, 1)
                                wait(dve, mred_chain, b, count("mred", step, each=4, plus=n - 4))
                            part = lambda n: neg_max_parts[:, n, :, :]
                            chained(dve.tensor_reduce(neg_max[:, :, :], maxima[:, :, :, :], AX.X, ALU.max, negate=True), 1)
                            chained(dve.tensor_copy(part(0), neg_max[:, :, :]), 2)
                            chained(dve.tensor_tensor(neg_max[:, :, :], neg_max[:, :, :], part(0), ALU.subtract), 3)
                            chained(dve.tensor_copy(part(1), neg_max[:, :, :]), 4)
                            dve.tensor_tensor(part(2), neg_max[:, :, :], part(1), ALU.subtract).then_inc(s["mred"], 1)
                        if kind in ("rest1", "part2"):
                            _, g, which, c = step
                            cols, m = slice(c * 512, (c + 1) * 512), "qk".index(which)
                            if kind == "rest1":
                                wait(dve, s["aux_act"], b, count("aux_act", (which, g, c)))
                                dst, minus = full[:, cols], parts[m][:, 0, cols]
                            else:
                                wait(dve, s["part1"], b, count("part1", ("part1", g, which, c)))
                                dst, minus = parts[m][:, 2, cols], parts[m][:, 1, cols]
                            dve.tensor_tensor(dst, full[:, cols], minus, ALU.subtract).then_inc(s[kind], 1)
                        if kind == "stats":
                            wait(dve, s["aux_dve"], b, count("aux_dve", ("op", step[1])))
                            for ii in range(2):
                                tile = (b - 1) * NT + 2 * step[1] + ii
                                dve.bn_stats(stats[:, bass.ds(tile, 1), :].rearrange("p a c -> p (a c)"),
                                             x_sb[:, bass.ds(tile, 1), :].rearrange("p a d -> p (a d)"))
                        if kind == "gmul":
                            wait(dve, s["aux_act"], b, count("aux_act", ("gate", NT // 2 - 1), back=1))
                            wait(dve, s["aux_dve"], b, count("aux_dve", ("ot", 3, 1)))
                            dve.scalar_tensor_tensor(out=flat[:, :, :], in0=gate[:, :, :], scalar=1.0, in1=flat[:, :, :],
                                                     op0=ALU.add, op1=ALU.mult).then_inc(s["gmul"], 1)
                        if kind not in AUX_DVE:
                            continue
                        src = aux_ps[bank(b, step)]
                        if kind == "mx":
                            wait_alone(dve, s["aux"], b, count("aux", step), passed)
                        else:
                            wait(dve, s["aux"], b, count("aux", step))
                        if kind == "zt":
                            i2 = step[1]
                            ins = dve.tensor_copy(
                                zT[:, :, i2 * 2 * P:(i2 + 1) * 2 * P].rearrange("p k (i q) -> p i k q", q=P),
                                src[:, :].rearrange("p (i k q) -> p i k q", i=2, k=KD))
                        elif kind == "v":
                            for ii in range(2):
                                ins = dve.tensor_tensor(v1[:, 2 * step[1] + ii, :, 0:HD],
                                                        src[:, ii * D:(ii + 1) * D].rearrange("p (h d) -> p h d", d=HD),
                                                        bv[:, :].rearrange("p (h d) -> p h d", d=HD), ALU.add)
                        elif kind == "mx":
                            _, g, h, i, c = step
                            if banded:
                                wid, mask = min(SPAN, (i + 1) * P), bias_q[:, HG * (g % G) + h, :]
                            else:
                                wid, mask = min(512, (i + 1) * P - 512 * c), causal[:, :]
                            if not banded and i >= 4 and c == 0:
                                ins = dve.tensor_reduce(maxima[:, h, i, c:c + 1], src[:, :], AX.X, ALU.max)
                            else:
                                ins = dve.tensor_tensor_reduce(src[:, 0:wid], src[:, 0:wid], mask[:, SPAN - wid:SPAN],
                                                               1.0, LOWEST, ALU.add, ALU.max, maxima[:, h, i, c:c + 1])
                        elif kind == "mt":
                            g = step[1]
                            wait(dve, mrows_in, b, count("mrow", ("mrow", G if g == 1 else g - 1), back=1 if g == 1 else 0, each=MROW))
                            ins = dve.tensor_copy(neg_max_rows[:, :], src[:, :].bitcast(BF16)[0:PARTS * HG * NT, 0:P])
                        elif kind == "ot":
                            _, g, c = step
                            o = src[:, :].rearrange("p (i h d) -> p i h d", i=4, h=HG)
                            ins = dve.reciprocal(recip[:, c, :, :], o[:, :, :, HD])
                            ins.then_inc(dve_chain, 1)
                            wait(dve, dve_chain, b, count("ot", step))
                            ins = dve.tensor_tensor(
                                flat[:, 4 * c:4 * c + 4, g * HG * HD:(g + 1) * HG * HD].rearrange("p i (h d) -> p i h d", d=HD),
                                o[:, :, :, 0:HD], recip[:, c, :, :].unsqueeze(3).to_broadcast([P, 4, HG, HD]), ALU.mult)
                        elif kind == "op":
                            tile = (b - 1) * NT + 2 * step[1]
                            xt = x_sb[:, bass.ds(tile, 2), :]
                            ins = dve.scalar_tensor_tensor(out=xt, in0=src[:, :].rearrange("p (i d) -> p i d", i=2),
                                                           scalar=0.5 if banded else 1.0, in1=xt, op0=ALU.mult, op1=ALU.add)
                        ins.then_inc(s["aux_dve"], 1)
                batches(dve, emit)

            @block.scalar
            def _(act):
                def emit(b):
                    for step in steps(b):
                        kind = step[0]
                        if kind == "S":
                            _, g, h, j, c = step
                            n = order.index(j) * HG + h
                            src, lo, wid = piece(b, step)
                            dst = probs[n % NP][:, lo:lo + wid]
                            if banded:
                                wait(act, added, b, count("S", step))
                                src = dst
                            else:
                                wait(act, s["S"], b, count("S", step))
                                if c == 0:
                                    wait(act, s["PV"], b, count("PV", ("PV", g, h, j), minus=NP))
                                src = src[:, 0:wid]
                            act.activation(dst, src, ACT.Exp).then_inc(probs_ready, 1)
                        elif kind == "ote":
                            g = step[1]
                            wait(act, s["PV"], b, count("PV", ("PV", g, HG - 1, order[-1])))
                            wait(act, s["aux"], b, count("aux", ("ot", (g - 1) % G, 1)))
                            act.activation(outT[:, :], outT_ps[:, :], ACT.Copy).then_inc(s["ote"], 1)
                        elif kind in ("q", "k"):
                            _, g, c = step
                            m = 0 if kind == "q" else 1
                            wait(act, s["aux"], b, count("aux", step))
                            back = 1 if kind == "q" and g == 2 else 0
                            before = (G if back else g if kind == "k" else 2, "q" if kind == "k" else "k")
                            wait(act, s["part2"], b, count("part2", ("part2",) + before + (c,), back=back))
                            wait(act, spilled, b, count("spill", ("spill", G if g == 2 else 2, kind), back=1 if g == 2 else 0, each=SPILL))
                            for dst in (parts[m][:, 0, c * 512:(c + 1) * 512], full[:, c * 512:(c + 1) * 512]):
                                ins = act.activation(dst, aux_ps[bank(b, step)][:, :], ACT.Identity,
                                                     bias=bqk[:, m, g // 2 % 2:g // 2 % 2 + 1], scale=HD ** -0.5 if m == 0 else 1.0)
                            ins.then_inc(s["aux_act"], 1)
                        elif kind == "part1":
                            _, g, which, c = step
                            wait(act, s["rest1"], b, count("rest1", ("rest1", g, which, c)))
                            act.activation(parts["qk".index(which)][:, 1, c * 512:(c + 1) * 512],
                                           full[:, c * 512:(c + 1) * 512], ACT.Copy).then_inc(s["part1"], 1)
                        elif kind == "at":
                            wait(act, s["aux"], b, count("aux", step))
                            act.activation(flatT[:, step[1] % 2, :], aux_ps[bank(b, step)][:, :], ACT.Copy).then_inc(s["aux_act"], 1)
                        elif kind in AUX_ACT:
                            i2 = step[1]
                            src = aux_ps[bank(b, step)][:, :]
                            wait(act, s["aux"], b, count("aux", step))
                            if kind == "zt":
                                ins = act.activation(
                                    zT[:, :, i2 * 2 * P:(i2 + 1) * 2 * P].rearrange("p k (i q) -> p i k q", q=P),
                                    src.rearrange("p (i k q) -> p i k q", i=2, k=KD), ACT.Copy)
                            elif kind == "v":
                                ins = act.activation(v1[:, 2 * i2:2 * i2 + 2, :, 0:HD],
                                                     src.rearrange("p (i h d) -> p i h d", i=2, d=HD), ACT.Copy)
                            else:
                                ins = act.activation(gate[:, 2 * i2:2 * i2 + 2, :], src.rearrange("p (i d) -> p i d", i=2),
                                                     ACT.Tanh, scale=0.5)
                            ins.then_inc(s["aux_act"], 1)

                batches(act, emit)

            @block.gpsimd
            def _(pool):
                def emit(b):
                    for step in steps(b):
                        kind = step[0]
                        if kind == "S" and not banded and step[4] == 0:
                            _, g, h, j, _ = step
                            n = order.index(j) * HG + h
                            wait_alone(pool, probs_ready, b, count("S", step), passed)
                            tri = probs[n % NP][:, 0:P]
                            pool.affine_select(out=tri, in_=tri, compare_op=ALU.is_ge, fill=0.0, base=0,
                                               pattern=[[1, P]], channel_multiplier=-1).then_inc(masked, 1)

                batches(pool, emit)

            @block.sync
            def _(sp):
                def emit(b):
                    for step in steps(b):
                        kind = step[0]
                        if kind == "bias":
                            g = step[1]
                            last = ("S", (g - 2) % G, HG - 1, order[-1], pieces(banded, order[-1]) - 1)
                            wait_alone(sp, added, b, count("S", last, back=1 if g == 1 else 0), passed)
                            sp.dma_start(bias_k[g % 2][:, :, :], windows(scratch["line_k"].ap(), HG * (g % G), HG)).then_inc(bias_in, 16)
                        elif kind == "spill":
                            _, g, which = step
                            wait_alone(sp, s["part2"], b, count("part2", ("part2", g, which, 1)), passed)
                            wait_alone(sp, stacked, b, count("stack", ("stack", 3 if g == 2 else 1), back=1 if g == 2 else 0, each=STACK), passed)
                            m = "qk".index(which)
                            for part in range(PARTS):
                                sp.dma_start(scratch["parts"].ap()[m, g // 2 % 2, :, part], parts[m][:, part, :]).then_inc(spilled, 16)
                        elif kind == "stack":
                            g = step[1]
                            even = g - g % 2
                            if even:
                                wait_alone(sp, spilled, b, count("spill", ("spill", even, "k"), each=SPILL), passed)
                            else:
                                wait_alone(sp, spilled, b, count("spill", ("spill", G, "k"), back=1, each=SPILL), passed)
                            last = ("S", (g - 2) % G, HG - 1, order[-1], pieces(banded, order[-1]) - 1)
                            wait_alone(sp, s["S"], b, count("S", last, back=1 if g == 1 else 0), passed)
                            for which, stack in enumerate((q_stack, k_stack)):
                                for row, part, parts_n in runs(which):
                                    src = scratch["parts"].ap()[which, g // 2 % 2, g % 2 * HG:(g % 2 + 1) * HG, part:part + parts_n]
                                    sp.dma_start(stack[g % 2][row * HD:(row + parts_n) * HD, :, :],
                                                 src.rearrange("h a d n -> (a d) h n")).then_inc(stacked, 16)
                        elif kind == "mrow":
                            g = step[1]
                            wait_alone(sp, s["aux_dve"], b, count("aux_dve", ("mt", g)), passed)
                            sp.dma_start(q_stack[g % 2][QK_ROWS:ALL_ROWS, :, :], neg_max_rows[:, :]).then_inc(mrows_in, 16)

                batches(sp, emit)

            @block.tensor
            def _(pe):
                pe.wait_ge(cleared, 5)

                def free_slot(b, step):
                    who, of = slot_free(step)
                    c = who(b if isinstance(b, int) else 1)
                    if c is None:
                        return
                    assert isinstance(b, int) or who(2) == c
                    wait(pe, s[c], b, of)

                def emit(b):
                    for step in steps(b):
                        kind = step[0]
                        if kind in AUX_DVE + AUX_ACT:
                            free_slot(b, step)
                            dst = aux_ps[bank(b, step)]
                        if kind == "S":
                            _, g, h, j, _ = step
                            n = order.index(j) * HG + h
                            if n == 0:
                                wait(pe, mrows_in, b, count("mrow", ("mrow", g or G), back=0 if g else 1, each=MROW))
                            wait(pe, added if banded else probs_ready, b, count("S", step, minus=tile_before(step)))
                            dst, lo, wid = piece(b, step)
                            pe.matmul(dst[:, 0:wid], k_stack[g % 2][:, h, j * P:(j + 1) * P],
                                      q_stack[g % 2][:, h, j * P + lo:j * P + lo + wid], start=True, stop=True).then_inc(s["S"], 1)
                        elif kind == "PV":
                            _, g, h, j = step
                            n = order.index(j) * HG + h
                            like = ("S", g, h, j, pieces(banded, j) - 1)
                            if n == 0:
                                if g:
                                    wait(pe, s["ote"], b, count("ote", ("ote", g - 1)))
                                else:
                                    wait(pe, s["ote"], b, count("ote", ("ote", G - 1), back=1))
                                    wait(pe, s[taker("v")], b, count(taker("v"), ("v", NT // 2 - 1)))
                            if not banded:
                                wait(pe, masked, b, count("PV", step))
                            if banded or like[4]:
                                wait(pe, probs_ready, b, count("S", like))
                            lo, hi = j * P, j * P + width(j)
                            while lo < hi:
                                top = min(hi, (lo // 512 + 1) * 512)
                                first = j == (0 if (lo < 512 or not banded) else 1)
                                ins = pe.matmul(outT_ps[32 * h:32 * h + HD + 1, lo:top], v1[:, j, HG * g + h, :],
                                                probs[n % NP][:, lo - j * P:top - j * P], start=first, stop=j == order[-1],
                                                skip_group_check=True)
                                lo = top
                            ins.then_inc(s["PV"], 1)
                        elif kind == "zt":
                            i2 = step[1]
                            wait(pe, s["z"], b, count("z", ("z", i2)))
                            for ii in range(2):
                                for kd in range(KD):
                                    ins = pe.transpose(dst[:, (ii * KD + kd) * P:(ii * KD + kd + 1) * P],
                                                       zb[:, i2 % 2, ii, kd * P:(kd + 1) * P], ident[:, :])
                            ins.then_inc(s["aux"], 1)
                        elif kind in ("q", "k"):
                            _, g, c = step
                            if g == G:
                                wait(pe, s[taker("zt")], b, count(taker("zt"), ("zt", NT // 2 - 1)))
                            for kd in range(KD):
                                ins = pe.matmul(dst[:, :], wqk[:, 0 if kind == "q" else 1, kd, g * HG % H:g * HG % H + 8, :].rearrange("p h d -> p (h d)"),
                                                zT[:, kd, c * 512:(c + 1) * 512], start=kd == 0, stop=kd == KD - 1)
                            ins.then_inc(s["aux"], 1)
                        elif kind in ("v", "gate"):
                            i2 = step[1]
                            for ii in range(2):
                                tile = slice((2 * i2 + ii) * P, (2 * i2 + ii + 1) * P)
                                for kd in range(KD):
                                    rhs = wv[:, kd, :, :].rearrange("p h d -> p (h d)") if kind == "v" else wgate[:, kd, :]
                                    ins = pe.matmul(dst[:, ii * D:(ii + 1) * D], zT[:, kd, tile], rhs,
                                                    start=kd == 0, stop=kd == KD - 1 and not banded)
                                if banded:
                                    bias = bv if kind == "v" else bgate
                                    ins = pe.matmul(dst[:, ii * D:(ii + 1) * D], ones_row[:, :], bias[:, :], start=False, stop=True)
                            ins.then_inc(s["aux"], 1)
                        elif kind == "mx":
                            _, g, h, i, c = step
                            if h == 0 and i == 0:
                                wait(pe, stacked, b, count("stack", ("stack", g), each=STACK))
                            if banded:
                                k0, wid = max(0, (i + 1) * P - SPAN), min(SPAN, (i + 1) * P)
                            else:
                                k0, wid = 512 * c, min(512, (i + 1) * P - 512 * c)
                            pe.matmul(dst[:, 0:wid], q_stack[g % 2][0:QK_ROWS, h, i * P:(i + 1) * P], k_stack[g % 2][0:QK_ROWS, h, k0:k0 + wid],
                                      start=True, stop=True).then_inc(s["aux"], 1)
                        elif kind == "mt":
                            wait(pe, s["mred"], b, count("mred", ("mred", step[1])))
                            pe.transpose(dst[:, :].bitcast(BF16)[0:PARTS * HG * NT, 0:P],
                                         neg_max_parts[:, :, :, :].rearrange("p a h i -> p (a h i)"), ident16[:, :]).then_inc(s["aux"], 1)
                        elif kind == "ot":
                            _, g, c = step
                            wait(pe, s["ote"], b, count("ote", ("ote", g), back=1 if g == G - 1 else 0))
                            for i in range(4):
                                ins = pe.transpose(dst[:, i * P:(i + 1) * P], outT[:, (4 * c + i) * P:(4 * c + i + 1) * P], ident[:, :])
                            ins.then_inc(s["aux"], 1)
                        elif kind == "at":
                            i2 = step[1]
                            if i2 == 0:
                                if banded:
                                    wait(pe, s["gmul"], b, count("gmul", ("gmul",)))
                                else:
                                    wait(pe, s["aux_dve"], b, count("aux_dve", ("ot", 3, 1)))
                            for ii in range(2):
                                for kd in range(KD):
                                    ins = pe.transpose(dst[:, (ii * KD + kd) * P:(ii * KD + kd + 1) * P],
                                                       flat[:, 2 * i2 + ii, kd * P:(kd + 1) * P], ident[:, :])
                            ins.then_inc(s["aux"], 1)
                        elif kind == "op":
                            i2 = step[1]
                            wait(pe, s["aux_act"], b, count("aux_act", ("at", i2)))
                            for ii in range(2):
                                for kd in range(KD):
                                    pe.matmul(dst[:, ii * D:(ii + 1) * D], flatT[:, i2 % 2, (ii * KD + kd) * P:(ii * KD + kd + 1) * P],
                                              wout[:, kd, :], start=kd == 0, stop=False)
                                ins = pe.matmul(dst[:, ii * D:(ii + 1) * D], ones_row[:, :], bout[:, :], start=False, stop=True)
                            ins.then_inc(s["aux"], 1)

                batches(pe, emit)



SLOTS = 4
QUADS = NE // 4


def ffn(nc, x_sb, stats, ident, w, scratch, tag, out=None):
    with ExitStack() as ctx:
        sb = lambda name, shape, dt=F32: ctx.enter_context(nc.sbuf_tensor(tag + name, shape, dt))
        sem = lambda name: ctx.enter_context(nc.semaphore(tag + name))
        mv = sb("mv", [P, B * NT, 2])
        rstd = sb("rstd", [P, B * NT])
        gate_wT = sb("gate_wT", [P, KD, NE])
        gate_b = sb("gate_b", [P, 1])
        b1T = sb("b1T", [P, HE // P, NE])
        b2 = sb("b2", [P, D])
        wT = sb("wT", [P, 2, N])
        wtok = sb("wtok", [P, NT, 2, P])
        mergedT = sb("mergedT", [P, KD, NE, B])
        w1_ring = sb("w1_ring", [P, SLOTS, KD, HE])
        w2_ring = sb("w2_ring", [P, SLOTS, HE // P, D])
        w1_in = [sem(f"w1_in{n}") for n in range(SLOTS)]
        w2_in = [sem(f"w2_in{n}") for n in range(SLOTS)]
        o_experts = sb("o_experts", [P, QUADS, D])
        o_batch = sb("o_batch", [P, 2, D])
        bank = [ctx.enter_context(nc.psum_tensor(f"{tag}ps{n}", [P, 512], F32)) for n in range(8)]

        def load_w1(eng, e, n):
            eng.dma_start(w1_ring[:, n, :, :], w["w1"][bass.ds(e, 1), 0:D, :].rearrange("a (p k) h -> p (a k) h", k=KD)
                          ).then_inc(w1_in[n], 16)

        def load_w2(eng, e, n):
            eng.dma_start(w2_ring[:, n, :, :], w["w2"][bass.ds(e, 1), 0:HE, :].rearrange("a (p c) d -> p (a c) d", c=HE // P)
                          ).then_inc(w2_in[n], 16)

        with ExitStack() as setup:
            ssb = lambda name, shape: setup.enter_context(nc.sbuf_tensor(tag + name, shape, F32))
            std = ssb("std", [P, B * NT])
            b1 = ssb("b1", [NE, HE])
            gw = ssb("gw", [NE, D])
            small_in, stat_steps, std_ready, turned, copied = (
                setup.enter_context(nc.semaphore(tag + n)) for n in ("small_in", "stat_steps", "std_ready", "turned", "copied"))
            with nc.Block() as block:
                @block.sync
                def _(sp):
                    sp.dma_start(b1[:, :], w["w1"][:, D, :]).then_inc(small_in, 16)
                    sp.dma_start(gw[:, :], w["gate_w"]).then_inc(small_in, 16)
                    for q in range(4):
                        sp.dma_start(b2[32 * q:32 * q + NE, :], w["w2"][:, HE, :]).then_inc(small_in, 16)
                        with nc.allow_non_contiguous_dma(reason="32 biases"):
                            sp.dma_start(gate_b[32 * q:32 * q + NE, :], w["gate_b"].rearrange("(e a) -> e a", a=1)).then_inc(small_in, 16)
                    for n in range(SLOTS):
                        load_w1(sp, n, n)
                        load_w2(sp, n, n)

                @block.scalar
                def _(act):
                    act.wait_ge(stat_steps, STATS_STEPS)
                    act.activation(std[:, :], std[:, :], ACT.Sqrt).then_inc(std_ready, 1)

                @block.tensor
                def _(pe):
                    pe.wait_ge(small_in, 160)
                    for c in range(HE // P):
                        pe.transpose(bank[0][:, c * NE:(c + 1) * NE], b1[:, c:HE:HE // P], ident[0:NE, 0:NE])
                    for kd in range(KD):
                        ins = pe.transpose(bank[1][:, kd * NE:(kd + 1) * NE], gw[:, kd * P:(kd + 1) * P], ident[0:NE, 0:NE])
                    ins.then_inc(turned, 1)

                @block.vector
                def _(dve):
                    layer_norm_stats(dve, std_ready, stat_steps, stats, mv, std, rstd)
                    dve.wait_ge(turned, 1)
                    dve.tensor_copy(b1T[:, :, :].rearrange("p c e -> p (c e)"), bank[0][:, 0:HE // P * NE]).then_inc(copied, 1)
                    dve.tensor_copy(gate_wT[:, :, :].rearrange("p k e -> p (k e)"), bank[1][:, 0:KD * NE]).then_inc(copied, 1)

        with ExitStack() as choose:
            ssb = lambda name, shape: choose.enter_context(nc.sbuf_tensor(tag + name, shape, F32))
            ssem = lambda name: choose.enter_context(nc.semaphore(tag + name))
            zb = ssb("zb", [P, 4, D])
            zT = ssb("zT", [P, 2, KD, 512])
            logits, marked = ssb("logits", [P, 2, N]), ssb("marked", [P, N])
            top, neg_max, total, inv = (ssb(n, [P, 2, m]) for n, m in (("top", TOPK), ("neg_max", 1), ("total", 1), ("inv", 1)))
            merged = ssb("merged", [P, 2, D])
            shift = ssb("shift", [P, B * NT])
            z_ready_act, shift_ready = ssem("z_ready_act"), ssem("shift_ready")
            z_ready, z_turned, zT_ready, logits_done, logits_ready = (
                ssem(n) for n in ("z_ready", "z_turned", "zT_ready", "logits_done", "logits_ready"))
            top_steps, exp_ready, w_ready, w_turned, wtok_ready = (
                ssem(n) for n in ("top_steps", "exp_ready", "w_ready", "w_turned", "wtok_ready"))
            merge_done, merged_ready, merged_turned = (ssem(n) for n in ("merge_done", "merged_ready", "merged_turned"))
            CH = B * NT // 4
            with nc.Block() as block:
                @block.tensor
                def _(pe):
                    def logit(c):
                        b, half = c // 2, c % 2
                        pe.wait_ge(zT_ready, c + 1)
                        if c >= 2:
                            pe.wait_ge(logits_ready, c - 1)
                        for kd in range(KD):
                            ins = pe.matmul(bank[2 + c % 2][32 * (b % 4):32 * (b % 4) + NE, :], gate_wT[:, kd, :],
                                            zT[:, c % 2, kd, :], start=kd == 0, stop=kd == KD - 1)
                        ins.then_inc(logits_done, 1)

                    for c in range(CH):
                        for ii in range(4):
                            t = 4 * c + ii
                            pe.wait_ge(z_ready, t + 1)
                            if t >= 8 and ii % 2 == 0:
                                pe.wait_ge(zT_ready, (t - 8) // 4 + 1)
                            for kd in range(KD):
                                ins = pe.transpose(bank[(0, 1, 4, 5)[t // 2 % 4]][:, (ii % 2 * KD + kd) * P:(ii % 2 * KD + kd + 1) * P],
                                                   zb[:, t % 4, kd * P:(kd + 1) * P], ident[:, :])
                            ins.then_inc(z_turned, 1)
                        if c:
                            logit(c - 1)
                    logit(CH - 1)
                    for gq in range(2):
                        pe.wait_ge(w_ready, gq + 1)
                        for half in range(2):
                            for ii in range(4):
                                i = 4 * half + ii
                                ins = pe.transpose(bank[4 * gq + half][:, ii * P:(ii + 1) * P], wT[:, gq, i * P:(i + 1) * P], ident[:, :])
                            ins.then_inc(w_turned, 1)
                    for t in range(B * NT):
                        b, i = t // NT, t % NT
                        if t == 0:
                            pe.wait_ge(wtok_ready, 4)
                        if t % 2:
                            pe.wait_ge(z_ready_act, t // 2 + 1)
                        else:
                            pe.wait_ge(z_ready, B * NT + t // 2 + 1)
                        q = b % 4
                        pe.matmul(bank[2 + b // 4][32 * q:32 * q + NE, 0:D], wtok[:, i, b // 4, 32 * q:32 * q + NE],
                                  zb[:, t % 4, :], start=i == 0, stop=i == NT - 1).then_inc(merge_done, 1)
                    pe.wait_ge(merged_ready, 2)
                    for gq in range(2):
                        for kd in range(KD):
                            ins = pe.transpose(bank[0][:, (gq * KD + kd) * P:(gq * KD + kd + 1) * P], merged[:, gq, kd:D:KD], ident[:, :])
                    ins.then_inc(merged_turned, 1)

                @block.scalar
                def _(act):
                    for c in range(CH):
                        if c >= 2:
                            act.wait_ge(logits_done, c - 1)
                        for pair in range(2):
                            act.wait_ge(z_turned, 4 * c + 2 * pair + 2)
                            ins = act.activation(
                                zT[:, c % 2, :, 2 * pair * P:2 * (pair + 1) * P].rearrange("p k (i q) -> p i k q", q=P),
                                bank[(0, 1, 4, 5)[(2 * c + pair) % 4]][:, :].rearrange("p (i k q) -> p i k q", i=2, k=KD), ACT.Copy)
                        ins.then_inc(zT_ready, 1)
                    for gq in range(2):
                        act.wait_ge(top_steps, 1 + 3 * gq + 1)
                        act.activation(wT[:, gq, :], logits[:, gq, :], ACT.Exp, bias=neg_max[:, gq, :],
                                       accum_out=total[:, gq, :]).then_inc(exp_ready, 1)
                    for gq in range(2):
                        for half in range(2):
                            act.wait_ge(w_turned, 2 * gq + half + 1)
                            act.activation(wtok[:, 4 * half:4 * half + 4, gq, :],
                                           bank[4 * gq + half][:, :].rearrange("p (i q) -> p i q", q=P), ACT.Copy).then_inc(wtok_ready, 1)
                    act.wait_ge(shift_ready, 1)
                    for t in range(1, B * NT, 2):
                        if t >= 4:
                            act.wait_ge(merge_done, t - 3)
                        act.activation(zb[:, t % 4, :], x_sb[:, t, :], ACT.Identity, bias=shift[:, t:t + 1],
                                       scale=rstd[:, t:t + 1]).then_inc(z_ready_act, 1)

                @block.vector
                def _(dve):
                    def z_tile(t):
                        dve.tensor_scalar(zb[:, t % 4, :], x_sb[:, t, :], mv[:, t, 0:1], rstd[:, t:t + 1],
                                          ALU.subtract, ALU.mult).then_inc(z_ready, 1)

                    def logits_of(c):
                        b, half = c // 2, c % 2
                        rows = slice(32 * (b % 4), 32 * (b % 4) + NE)
                        dve.wait_ge(logits_done, c + 1)
                        dve.tensor_scalar(logits[rows, b // 4, half * 512:(half + 1) * 512], bank[2 + c % 2][rows, :],
                                          gate_b[rows, :], None, ALU.add).then_inc(logits_ready, 1)

                    dve.scalar_tensor_tensor(out=shift[:, :], in0=mv[:, :, 0], scalar=-1.0, in1=rstd[:, :],
                                             op0=ALU.mult, op1=ALU.mult).then_inc(shift_ready, 1)
                    for c in range(CH):
                        for t in range(4 * c, 4 * c + 4):
                            if t >= 4:
                                dve.wait_ge(z_turned, t - 3)
                            z_tile(t)
                        if c >= 2:
                            logits_of(c - 2)
                    logits_of(CH - 2)
                    logits_of(CH - 1)
                    dve.wait_ge(logits_ready, CH)
                    for gq in range(2):
                        dve.max(top[:, gq, :], logits[:, gq, :]).then_inc(top_steps, 1)
                        dve.wait_ge(top_steps, 3 * gq + 1)
                        dve.tensor_scalar(neg_max[:, gq, :], top[:, gq, 0:1], -1.0, None, ALU.mult).then_inc(top_steps, 1)
                        if gq:
                            dve.wait_ge(w_ready, gq)
                        dve.match_replace(marked[:, :], top[:, gq, :], logits[:, gq, :], LOWEST).then_inc(top_steps, 1)
                        dve.wait_ge(exp_ready, gq + 1)
                        dve.wait_ge(top_steps, 3 * gq + 3)
                        dve.reciprocal(inv[:, gq, :], total[:, gq, :]).then_inc(logits_ready, 1)
                        dve.scalar_tensor_tensor(out=wT[:, gq, :], in0=marked[:, :], scalar=LOWEST, in1=wT[:, gq, :],
                                                 op0=ALU.is_equal, op1=ALU.mult).then_inc(logits_ready, 1)
                        dve.wait_ge(logits_ready, CH + 2 * gq + 2)
                        dve.tensor_scalar(wT[:, gq, :], wT[:, gq, :], inv[:, gq, :], None, ALU.mult).then_inc(w_ready, 1)
                    for t in range(0, B * NT, 2):
                        if t >= 4:
                            dve.wait_ge(merge_done, t - 3)
                        z_tile(t)
                    dve.wait_ge(merge_done, B * NT)
                    for gq in range(2):
                        dve.tensor_copy(merged[:, gq, :], bank[2 + gq][:, 0:D]).then_inc(merged_ready, 1)
                    dve.wait_ge(merged_turned, 1)
                    for gq in range(2):
                        for kd in range(KD):
                            c0 = (gq * KD + kd) * P
                            dve.tensor_copy(mergedT[:, kd, :, 4 * gq:4 * gq + 4],
                                            bank[0][:, c0:c0 + P].rearrange("p (b e) -> p e b", e=NE)).then_inc(logits_ready, 1)

        with ExitStack() as run:
            rsb = lambda name, shape: run.enter_context(nc.sbuf_tensor(tag + name, shape, F32))
            rsem = lambda name: run.enter_context(nc.semaphore(tag + name))
            lhs1 = [rsb(f"lhs1_{n}", [P, KD, 4, 32]) for n in range(2)]
            hid = [rsb(f"hid{n}", [P, HE]) for n in range(2)]
            hidT = [rsb(f"hidT{n}", [P, HE // P, 4, 32]) for n in range(2)]
            pre = rsb("pre", [P, HE // P, 4, B])
            cleared, lhs1_ready, hid_done, hid_ready, hid_turned, pre_ready, hidT_ready, out_done, out_ready, moved = (
                rsem(n) for n in ("cleared", "lhs1_ready", "hid_done", "hid_ready", "hid_turned", "pre_ready",
                                  "hidT_ready", "out_done", "out_ready", "moved"))
            scattered, summed, o_ready, kept, stored = (rsem(n) for n in ("scattered", "summed", "o_ready", "kept", "stored"))

            with nc.Block() as block:
                def pairs(eng, emit):
                    emit(0)
                    with eng.Fori(1, QUADS // 2 - 1) as it:
                        emit(it)
                    emit(QUADS // 2 - 1, last=True)

                @block.sync
                def _(sp):
                    def next_w1(q):
                        for j in range(4):
                            sp.wait_ge(hid_done, q * 4 + j + 1)
                            load_w1(sp, q * 4 + j + SLOTS, j)

                    def next_w2(q):
                        for j in range(4):
                            sp.wait_ge(out_done, q * 4 + j + 1)
                            load_w2(sp, q * 4 + j + SLOTS, j)

                    def keep_outputs(q):
                        sp.wait_ge(out_ready, q + 1)
                        for j in range(4):
                            sp.dma_start(scratch["outputs"].ap()[:, bass.ds(q * 4 + j, 1), :],
                                         o_experts[32 * j:32 * j + B, bass.ds(q, 1), :]).then_inc(kept, 16)

                    next_w1(0)
                    with sp.Fori(1, QUADS - 1) as q:
                        next_w1(q)
                        next_w2(q - 1)
                        keep_outputs(q - 1)
                    next_w2(QUADS - 2)
                    keep_outputs(QUADS - 2)
                    keep_outputs(QUADS - 1)
                    sp.wait_ge(kept, 16 * NE)
                    for gq in range(2):
                        sp.dma_start(o_batch[:, gq, :], scratch["outputs"].ap()[4 * gq:4 * gq + 4].rearrange("b e d -> (b e) d")
                                     ).then_inc(moved, 16)
                    if out is not None:
                        for b in range(B):
                            sp.wait_ge(summed, (b + 1) * NT // 2)
                            sp.dma_start(out[b].rearrange("(i p) d -> p i d", p=P), x_sb[:, b * NT:(b + 1) * NT, :]).then_inc(stored, 16)
                        sp.wait_ge(stored, 16 * B)

                @block.gpsimd
                def _(pool):
                    for n in range(2):
                        pool.memset(lhs1[n][:, :, :, :], 0.0).then_inc(cleared, 1)
                        pool.memset(hidT[n][:, :, :, :], 0.0).then_inc(cleared, 1)
                    pool.wait_ge(cleared, 4)

                    def emit(it, last=False):
                        for half in range(2):
                            wait(pool, hid_done, it, lambda i: 4 * (2 * i + half - 1) if 2 * i + half >= 2 else None)
                            pool.tensor_copy(lhs1[half][:, :, :, 0:B],
                                             mergedT[:, :, bass.ds(it * 8 + 4 * half, 4), :]).then_inc(lhs1_ready, 1)
                    pairs(pool, emit)

                @block.tensor
                def _(pe):
                    pe.wait_ge(cleared, 4)

                    def up(it, half, ahead=0):
                        quad = lambda i: 2 * (i + ahead) + half
                        wait(pe, lhs1_ready, it, lambda i: quad(i) + 1)
                        wait(pe, hid_ready, it, lambda i: quad(i) or None)
                        for j in range(4):
                            wait(pe, w1_in[j], it, lambda i: 16 * (quad(i) + 1))
                            for n in range(2):
                                for kd in range(KD):
                                    ins = pe.matmul(bank[n][32 * j:32 * j + 32, :], lhs1[half][:, kd, j, :],
                                                    w1_ring[:, j, kd, n * 512:(n + 1) * 512], start=kd == 0, stop=kd == KD - 1)
                            ins.then_inc(hid_done, 1)

                    def turn(it, half):
                        wait(pe, hid_ready, it, lambda i: 2 * i + half + 1)
                        wait(pe, pre_ready, it, lambda i: 2 * i + half if 2 * i + half else None)
                        for c in range(HE // P):
                            ins = pe.transpose(bank[2 + c // 4][:, c % 4 * P:(c % 4 + 1) * P], hid[half][:, c:HE:HE // P], ident[:, :])
                        ins.then_inc(hid_turned, 1)

                    def down(it, half):
                        wait(pe, hidT_ready, it, lambda i: 2 * i + half + 1)
                        if half == 0:
                            wait(pe, out_ready, it, lambda i: 2 * i - 1 if i else None)
                        else:
                            wait(pe, out_ready, it, lambda i: 2 * i if i else None)
                        for j in range(4):
                            wait(pe, w2_in[j], it, lambda i: 16 * (2 * i + half + 1))
                            for c in range(HE // P):
                                ins = pe.matmul(bank[4 + half][32 * j:32 * j + 32, 0:D], hidT[half][:, c, j, :],
                                                w2_ring[:, j, c, :], start=c == 0, stop=c == HE // P - 1)
                            ins.then_inc(out_done, 1)

                    def emit(it, last=False):
                        turn(it, 0)
                        up(it, 1)
                        down(it, 0)
                        turn(it, 1)
                        if not last:
                            up(it, 0, ahead=1)
                        down(it, 1)
                    up(0, 0)
                    pairs(pe, emit)

                    pe.wait_ge(o_ready, 1)
                    for t2 in range(B * NT // 2):
                        if t2 >= 2:
                            pe.wait_ge(summed, t2 - 1)
                        for ii in range(2):
                            b, i = (2 * t2 + ii) // NT, (2 * t2 + ii) % NT
                            rows = slice(32 * (b % 4), 32 * (b % 4) + NE)
                            ins = pe.matmul(bank[6 + t2 % 2][:, ii * D:(ii + 1) * D], wT[rows, b // 4, i * P:(i + 1) * P],
                                            o_batch[rows, b // 4, :], start=True, stop=True)
                        ins.then_inc(scattered, 1)

                @block.scalar
                def _(act):
                    def take_hidden(it, half, ahead=0):
                        quad = lambda i: 2 * (i + ahead) + half
                        wait(act, hid_done, it, lambda i: 4 * (quad(i) + 1))
                        wait(act, hid_turned, it, lambda i: quad(i) - 1 if quad(i) >= 2 else None)
                        for n in range(2):
                            ins = act.activation(hid[half][:, n * 512:(n + 1) * 512], bank[n][:, :], ACT.Copy)
                        ins.then_inc(hid_ready, 1)

                    def gelu(it, half):
                        wait(act, pre_ready, it, lambda i: 2 * i + half + 1)
                        wait(act, out_done, it, lambda i: 4 * (2 * i + half - 1) if 2 * i + half >= 2 else None)
                        act.activation(hidT[half][:, :, :, 0:B], pre[:, :, :, :], ACT.Gelu).then_inc(hidT_ready, 1)

                    def take_outputs(it, half):
                        wait(act, out_done, it, lambda i: 4 * (2 * i + half + 1))
                        act.activation(o_experts[:, bass.ds(2 * it + half, 1), :].rearrange("p a d -> p (a d)"),
                                       bank[4 + half][:, 0:D], ACT.Copy).then_inc(out_ready, 1)

                    def emit(it, last=False):
                        gelu(it, 0)
                        take_hidden(it, 1)
                        take_outputs(it, 0)
                        gelu(it, 1)
                        if not last:
                            take_hidden(it, 0, ahead=1)
                        take_outputs(it, 1)
                    take_hidden(0, 0)
                    pairs(act, emit)

                @block.vector
                def _(dve):
                    def emit(it, last=False):
                        for half in range(2):
                            wait(dve, hid_turned, it, lambda i: 2 * i + half + 1)
                            wait(dve, hidT_ready, it, lambda i: 2 * i + half if 2 * i + half else None)
                            for n in range(2):
                                ins = dve.tensor_tensor(
                                    pre[:, 4 * n:4 * n + 4, :, :],
                                    bank[2 + n][:, :].rearrange("p (c j r) -> p c j r", c=4, j=4)[:, :, :, 0:B],
                                    b1T[:, 4 * n:4 * n + 4, bass.ds(it * 8 + 4 * half, 4)].unsqueeze(3).to_broadcast([P, 4, 4, B]), ALU.add)
                            ins.then_inc(pre_ready, 1)
                    pairs(dve, emit)
                    dve.wait_ge(moved, 32)
                    for gq in range(2):
                        ins = dve.tensor_tensor(o_batch[:, gq, :], o_batch[:, gq, :], b2[:, :], ALU.add)
                    ins.then_inc(o_ready, 1)
                    for t2 in range(B * NT // 2):
                        dve.wait_ge(scattered, t2 + 1)
                        xt = x_sb[:, 2 * t2:2 * t2 + 2, :].rearrange("p i d -> p (i d)")
                        dve.tensor_tensor(xt, bank[6 + t2 % 2][:, :], xt, ALU.add).then_inc(summed, 1)
                        if out is None:
                            dve.wait_ge(summed, t2 + 1)
                            for t in (2 * t2, 2 * t2 + 1):
                                dve.bn_stats(stats[:, t, :], x_sb[:, t, :])


def build(nc, a, out):
    scratch = {n: nc.dram_tensor(n + "_dram", [H, P, LINE], dt) for n, dt in (("line_k", F32), ("line_q", BF16))}
    scratch["parts"] = nc.dram_tensor("parts_dram", [2, 2, 8, PARTS, HD, N], BF16)
    attn_a = {"qkv": a["L0_attn_a_Wqkv"], "bqkv": a["L0_attn_a_bqkv"], "out": a["L0_attn_a_Wout"], "bout": a["L0_attn_a_bout"],
              "gate": a["L0_attn_a_Wgate"], "bgate": a["L0_attn_a_bgate"], "pos_bias": a["L0_attn_a_pos_bias"]}
    attn_b = {"qkv": a["L0_attn_b_W1"], "bqkv": a["L0_attn_b_b1"], "out": a["L0_attn_b_W2"], "bout": a["L0_attn_b_b2"]}
    experts = {"gate_w": a["L0_ffn_gate_w"], "gate_b": a["L0_ffn_gate_b"], "w1": a["L0_ffn_w1"], "w2": a["L0_ffn_w2"]}
    scratch["outputs"] = nc.dram_tensor("outputs_dram", [B, NE, D], F32)
    with (nc.sbuf_tensor("x_sb", [P, B * NT, D], F32) as x_sb, nc.sbuf_tensor("ident", [P, P], F32) as ident,
          nc.sbuf_tensor("stats", [P, B * NT, 6], F32) as stats):
        build_constants(nc, ident, a["L0_attn_a_x"], x_sb, stats)
        attention(nc, x_sb, stats, ident, attn_a, True, scratch)
        ffn(nc, x_sb, stats, ident, experts, scratch, "f1_")
        attention(nc, x_sb, stats, ident, attn_b, False, scratch)
        ffn(nc, x_sb, stats, ident, experts, scratch, "f2_", out)


_INS = ["L0_attn_a_x", "L0_attn_a_Wqkv", "L0_attn_a_bqkv", "L0_attn_a_Wout", "L0_attn_a_bout", "L0_attn_a_Wgate",
        "L0_attn_a_bgate", "L0_attn_a_pos_bias", "L0_attn_b_W1", "L0_attn_b_b1", "L0_attn_b_W2", "L0_attn_b_b2",
        "L0_ffn_gate_w", "L0_ffn_gate_b", "L0_ffn_w1", "L0_ffn_w2"]


def kernel(**inputs):
    import numpy as _np
    import concourse.bacc as _bacc
    from concourse import mybir as _mybir
    from concourse.bass_utils import run_bass_kernel_spmd as _run

    nc = _bacc.Bacc("TRN2", target_bir_lowering=False, num_devices=1, dynamic_dma_scratch_size=256)
    arrays, args = {}, {}
    for name in _INS:
        a = _np.ascontiguousarray(inputs[name])
        arrays[f"in_{name}_dram"] = a
        args[name] = nc.dram_tensor(f"in_{name}_dram", a.shape, _mybir.dt.from_np(a.dtype), kind="ExternalInput").ap()
    out = nc.dram_tensor("out_0_dram", (8, 1024, 256), _mybir.dt.float32, kind="ExternalOutput").ap()
    build(nc, args, out)
    r = _run(nc, [arrays], core_ids=[0])
    return r.results[0]["out_0_dram"]
```
